# Optimizing a Trainium2 kernel written in Bass

```python
import numpy as np
import jax
import jax.numpy as jnp

def _softmax(x, axis=-1):
    return jax.nn.softmax(x, axis=axis)

def _gelu(x):
    return jax.nn.gelu(x, approximate=True)

def _silu(x):
    return jax.nn.silu(x)

def _sigmoid(x):
    return jax.nn.sigmoid(x)

def _layernorm(x, axis=-1, eps=1e-05):
    m = jnp.mean(x, axis=axis, keepdims=True)
    v = jnp.var(x, axis=axis, keepdims=True)
    return (x - m) / jnp.sqrt(v + eps)

def _scatter_add(tgt, idx, src, axis=0):
    return tgt.at[idx].add(src)

def _segment_sum(src, seg, n):
    return jax.ops.segment_sum(src, seg, n)
kernel_name = 'mk_xattn_ffn_d1_seqx_r4_cbdfdf'

def setup_inputs(seed: int=0):
    np.random.seed(seed)
    _w = jnp.asarray

    def _rec_inputs():
        import jax
        import jax.numpy as jnp
        _rk = jax.random.key(seed)
        x = 7.22e-05 + 1 * jax.random.normal(jax.random.fold_in(_rk, 1), (4, 1024, 256), jnp.float32)
        _lenS = 1024 - jax.random.randint(jax.random.fold_in(_rk, 7), (4,), 0, max(1, 1024 // 4) + 1, jnp.int32)
        _lenS2 = 77 - jax.random.randint(jax.random.fold_in(_rk, 8), (4,), 0, max(1, 77 // 4) + 1, jnp.int32)
        _ctx_1024P = jax.random.normal(jax.random.fold_in(_rk, 11), (4, 16, 256), jnp.float32)
        _ctx_1024c = jax.random.dirichlet(jax.random.fold_in(_rk, 511), 0.3 * jnp.ones((16,), jnp.float32), (4, 77))
        _ctx_1024t = jnp.einsum('bsk,bkd->bsd', _ctx_1024c, _ctx_1024P)
        _ctx_1024t = _ctx_1024t * jax.lax.rsqrt(jnp.mean(jnp.square(_ctx_1024t)) + 1e-12) * 0.953939
        ctx_1024 = 4.13588e-05 + 0.999923 * (_ctx_1024t + 0.3 * jax.random.normal(jax.random.fold_in(_rk, 611), (4, 77, 256), jnp.float32))
        return (x, ctx_1024)
    x, ctx_1024 = _rec_inputs()

    def _L0_xattn_setup():
        import jax, jax.numpy as jnp
        import numpy as np
        D_MODEL = 256
        N_HEAD = 16
        D_K = 64
        D_V = 64
        LN_EPS = 0.001
        key = jax.random.key(seed)
        ks = jax.random.split(key, 10)
        B, S = (4, 512)
        scale_in = 1.0 / np.sqrt(D_MODEL)
        scale_attn = 1.0 / np.sqrt(D_V * N_HEAD)
        return {'q': jax.random.normal(ks[0], (B, S, D_MODEL), jnp.float32), 'k': jax.random.normal(ks[1], (B, S, D_MODEL), jnp.float32), 'v': jax.random.normal(ks[2], (B, S, D_MODEL), jnp.float32), 'Wq': jax.random.normal(ks[3], (D_MODEL, D_K * N_HEAD), jnp.float32) * scale_in, 'bq': jnp.zeros((D_K * N_HEAD,), jnp.float32), 'Wk': jax.random.normal(ks[4], (D_MODEL, D_K * N_HEAD), jnp.float32) * scale_in, 'bk': jnp.zeros((D_K * N_HEAD,), jnp.float32), 'Wv': jax.random.normal(ks[5], (D_MODEL, D_V * N_HEAD), jnp.float32) * scale_in, 'bv': jnp.zeros((D_V * N_HEAD,), jnp.float32), 'Wo': jax.random.normal(ks[6], (D_V * N_HEAD, D_MODEL), jnp.float32) * scale_attn, 'bo': jnp.zeros((D_MODEL,), jnp.float32), 'gamma': jnp.ones((D_MODEL,), jnp.float32), 'beta': jnp.zeros((D_MODEL,), jnp.float32)}
    _L0_xattn_all = _L0_xattn_setup()
    _L0_xattn_in = {k: v for k, v in _L0_xattn_all.items() if k in ('Wq', 'bq', 'Wk', 'bk', 'Wv', 'bv', 'Wo', 'bo', 'gamma', 'beta')}
    del _L0_xattn_all

    def _L0_ffn_setup():
        import jax, jax.numpy as jnp
        import numpy as np
        TOP_K = 4
        CAP_FACTOR = 4

        def swiglu(x, w1, w2, w3):
            return jax.nn.silu(x @ w1) * (x @ w3) @ w2
        key = jax.random.key(seed)
        ks = jax.random.split(key, 8)
        B, S, D, H, E = (2, 512, 256, 128, 32)
        Hs = 2 * H
        sd = lambda *sh: 1.0 / np.sqrt(sh[-2])
        x = jax.random.normal(ks[0], (B, S, D), dtype=jnp.float32)
        Wg = jax.random.normal(ks[1], (D, E), dtype=jnp.float32) * (1.0 / np.sqrt(D))
        W1 = jax.random.normal(ks[2], (E, D, H), dtype=jnp.float32) * (1.0 / np.sqrt(D))
        W3 = jax.random.normal(ks[3], (E, D, H), dtype=jnp.float32) * (1.0 / np.sqrt(D))
        W2 = jax.random.normal(ks[4], (E, H, D), dtype=jnp.float32) * (1.0 / np.sqrt(H))
        Ws1 = jax.random.normal(ks[5], (D, Hs), dtype=jnp.float32) * (1.0 / np.sqrt(D))
        Ws3 = jax.random.normal(ks[6], (D, Hs), dtype=jnp.float32) * (1.0 / np.sqrt(D))
        Ws2 = jax.random.normal(ks[7], (Hs, D), dtype=jnp.float32) * (1.0 / np.sqrt(Hs))
        return {'x': x, 'Wg': Wg, 'W1': W1, 'W2': W2, 'W3': W3, 'Ws1': Ws1, 'Ws2': Ws2, 'Ws3': Ws3}
    _L0_ffn_all = _L0_ffn_setup()
    _L0_ffn_in = {k: v for k, v in _L0_ffn_all.items() if k in ('Wg', 'W1', 'W2', 'W3', 'Ws1', 'Ws2', 'Ws3')}
    del _L0_ffn_all
    return {'x': x, 'ctx_1024': ctx_1024, 'L0_xattn_Wq': _L0_xattn_in['Wq'], 'L0_xattn_bq': _L0_xattn_in['bq'], 'L0_xattn_Wk': _L0_xattn_in['Wk'], 'L0_xattn_bk': _L0_xattn_in['bk'], 'L0_xattn_Wv': _L0_xattn_in['Wv'], 'L0_xattn_bv': _L0_xattn_in['bv'], 'L0_xattn_Wo': _L0_xattn_in['Wo'], 'L0_xattn_bo': _L0_xattn_in['bo'], 'L0_xattn_gamma': _L0_xattn_in['gamma'], 'L0_xattn_beta': _L0_xattn_in['beta'], 'L0_ffn_Wg': _L0_ffn_in['Wg'], 'L0_ffn_W1': _L0_ffn_in['W1'], 'L0_ffn_W2': _L0_ffn_in['W2'], 'L0_ffn_W3': _L0_ffn_in['W3'], 'L0_ffn_Ws1': _L0_ffn_in['Ws1'], 'L0_ffn_Ws2': _L0_ffn_in['Ws2'], 'L0_ffn_Ws3': _L0_ffn_in['Ws3']}

def reference(x, ctx_1024, L0_xattn_Wq, L0_xattn_bq, L0_xattn_Wk, L0_xattn_bk, L0_xattn_Wv, L0_xattn_bv, L0_xattn_Wo, L0_xattn_bo, L0_xattn_gamma, L0_xattn_beta, L0_ffn_Wg, L0_ffn_W1, L0_ffn_W2, L0_ffn_W3, L0_ffn_Ws1, L0_ffn_Ws2, L0_ffn_Ws3):
    import jax
    import jax.numpy as jnp

    def _L0_xattn_ref(q, k, v, Wq, bq, Wk, bk, Wv, bv, Wo, bo, gamma, beta):
        import jax, jax.numpy as jnp
        import numpy as np
        D_MODEL = 256
        N_HEAD = 16
        D_K = 64
        D_V = 64
        LN_EPS = 0.001
        B, Sq, _ = q.shape
        Sk = k.shape[1]
        qh = (q @ Wq + bq).reshape(B, Sq, N_HEAD, D_K).transpose(0, 2, 1, 3)
        kh = (k @ Wk + bk).reshape(B, Sk, N_HEAD, D_K).transpose(0, 2, 1, 3)
        vh = (v @ Wv + bv).reshape(B, Sk, N_HEAD, D_V).transpose(0, 2, 1, 3)
        scores = jnp.einsum('bhqd,bhkd->bhqk', qh, kh)
        probs = jax.nn.softmax(scores, axis=-1)
        attn = jnp.einsum('bhqk,bhkd->bhqd', probs, vh)
        attn = attn.transpose(0, 2, 1, 3).reshape(B, Sq, N_HEAD * D_V)
        out = attn @ Wo + bo
        x = q + out
        mean = jnp.mean(x, axis=-1, keepdims=True)
        var = jnp.var(x, axis=-1, keepdims=True)
        return gamma * (x - mean) * jax.lax.rsqrt(var + LN_EPS) + beta

    def _L0_ffn_ref(x, Wg, W1, W2, W3, Ws1, Ws2, Ws3):
        import jax, jax.numpy as jnp
        import numpy as np
        TOP_K = 4
        CAP_FACTOR = 4

        def swiglu(x, w1, w2, w3):
            return jax.nn.silu(x @ w1) * (x @ w3) @ w2
        B, S, D = x.shape
        E = Wg.shape[1]
        T = B * S
        xf = x.reshape(T, D)
        scores = jax.nn.softmax(xf @ Wg, axis=-1)
        weights, indices = jax.lax.top_k(scores, TOP_K)
        P = T * TOP_K
        pair_expert = indices.reshape(-1)
        pair_token = jnp.repeat(jnp.arange(T), TOP_K)
        pair_weight = weights.reshape(-1).astype(xf.dtype)
        C = CAP_FACTOR * P // E
        y = jnp.zeros_like(xf)
        for e in range(E):
            pos = jnp.nonzero(pair_expert == e, size=C, fill_value=P)[0]
            valid = pos < P
            safe = jnp.minimum(pos, P - 1)
            tok = jnp.where(valid, pair_token[safe], 0)
            w = jnp.where(valid, pair_weight[safe], 0.0)
            xg = xf[tok]
            out = swiglu(xg, W1[e], W2[e], W3[e]) * w[:, None]
            y = y.at[tok].add(out)
        z = swiglu(xf, Ws1, Ws2, Ws3)
        return (y + z).reshape(B, S, D)
    x = x + _L0_xattn_ref(_layernorm(x, axis=-1), ctx_1024, ctx_1024, L0_xattn_Wq, L0_xattn_bq, L0_xattn_Wk, L0_xattn_bk, L0_xattn_Wv, L0_xattn_bv, L0_xattn_Wo, L0_xattn_bo, L0_xattn_gamma, L0_xattn_beta)
    x = x + _L0_ffn_ref(_layernorm(x, axis=-1), L0_ffn_Wg, L0_ffn_W1, L0_ffn_W2, L0_ffn_W3, L0_ffn_Ws1, L0_ffn_Ws2, L0_ffn_Ws3)
    return x

_drawn_inputs = setup_inputs


def setup_inputs(seed=0):
    import zlib

    import numpy as np

    out = dict(_drawn_inputs(seed))
    spreads = {'L0_xattn_bq': (0.0, 0.1),
     'L0_xattn_bk': (0.0, 0.1),
     'L0_xattn_bv': (0.0, 0.1),
     'L0_xattn_bo': (0.0, 0.1),
     'L0_xattn_gamma': (1.0, 0.2),
     'L0_xattn_beta': (0.0, 0.1)}
    factors = {}
    for name, (base, spread) in spreads.items():
        noise = np.random.default_rng([zlib.crc32(name.encode()), seed]).standard_normal(out[name].shape)
        drawn = base * np.exp(spread * noise) if base else spread * noise
        out[name] = jnp.asarray(drawn.astype(out[name].dtype))
    for name, factor in factors.items():
        out[name] = (out[name] * factor).astype(out[name].dtype)
    return out
```

```python
from contextlib import ExitStack

import concourse.bass as bass
from concourse import mybir

F32 = mybir.dt.float32
BF16 = mybir.dt.bfloat16
I32 = mybir.dt.int32
U32 = mybir.dt.uint32
ALU = mybir.AluOpType
ACT = mybir.ActivationFunctionType
AX = mybir.AxisListType.X

P = 128
BANK = 512
RSQRT_SEED = 0x5F3759DF
NEWTON = 3
RSQRT_OPS = 3 + 3 * NEWTON


def attention_moe_kernel(nc, x, ctx, Wq, bq, Wk, bk, Wv, bv, Wo, bo, gamma, beta,
                         Wg, W1, W2, W3, Ws1, Ws2, Ws3, out):
    B, S, D = x.shape
    SK = ctx.shape[1]
    HD = Wq.shape[1]
    DH = 64
    NH = HD // DH
    E, _, H = W1.shape
    HS = Ws1.shape[1]
    TOPK = 4
    EPS_LN, EPS_ATT = 1e-5, 1e-3
    T = B * S
    KC = D // P
    HP = HD // P
    HK = NH * SK
    CK = (HK + P - 1) // P
    HKP = CK * P
    BK = B * SK
    SKE = SK + SK % 2
    TG = 4
    GT = TG * P
    NT = T // P
    NG = NT // TG
    CAP = 4 * T * TOPK // E
    REG = CAP + P
    DUMMY = E * REG
    TRASH = DUMMY + P
    ROW = D + 1 + E
    NACC = 4
    BLOCKS = -(-((T * TOPK + E * (P - 1)) // P) // (2 * NACC)) * 2 * NACC
    NX = 2 * NACC
    LAG = 3
    TURNS = BLOCKS // NX
    YROWS = T + P
    EW = 3 * D
    EARLY = 5
    assert NG == 2 * B and KC == 2 and HS == 2 * P and H == P and BLOCKS <= 2 * P and P % E == 0

    xt = x.rearrange("b s d -> (b s) d")
    ot = out.rearrange("b s d -> (b s) d")
    lists = nc.dram_tensor("expert_lists", [TRASH + P, ROW], F32, kind="Internal").ap()
    xn2T_d = nc.dram_tensor("xn2T_d", [NG, P, KC * GT], F32, kind="Internal").ap()
    acc = [nc.dram_tensor(f"acc{i}", [YROWS, D], F32, kind="Internal").ap() for i in range(NACC)]

    with ExitStack() as stack:
        def sb(name, shape, dt=F32, scope=stack):
            return scope.enter_context(nc.sbuf_tensor(name, shape, dt))

        def sem(name):
            return stack.enter_context(nc.semaphore(name))

        big = sb("big", [P, E * EW])
        ew = big[:, :].rearrange("p (e n) -> p e n", e=E)
        a_at = EARLY * EW
        vo_at = a_at + KC * B * HK
        A = big[:, a_at:vo_at].rearrange("p (k b n) -> p k b n", k=KC, b=B)
        VO = big[:, vo_at:vo_at + B * CK * D].rearrange("p (b c n) -> p b c n", b=B, c=CK)
        wq_sb = big[:, 0:KC * HD].rearrange("p (k n) -> p k n", k=KC)
        xs = big[:, KC * HD:KC * HD + TG * D].rearrange("p (t d) -> p t d", t=TG)
        assert KC * HD + TG * D <= a_at and vo_at + B * CK * D <= E * EW
        ident = sb("ident", [P, P])
        identb = sb("identb", [P, P], BF16)
        before = sb("before", [P, P], BF16)
        onesb = sb("onesb", [P, P], BF16)
        iota_e = sb("iota_e", [P, E])
        region = sb("region", [P, E])
        region0 = sb("region0", [P, E])
        trash_p = sb("trash_p", [P, 1])
        block_i = sb("block_i", [P, 2])
        bias3 = sb("bias3", [3, B, HK], BF16)
        ones3 = sb("ones3", [3, P], BF16)
        ln1 = sb("ln1", [P, NT, 2])
        wg = sb("wg", [P, KC, E])
        ws13 = sb("ws13", [P, KC, 2 * HS])
        ws2 = sb("ws2", [P, KC, D])
        gamma_b = sb("gamma_b", [P, D])
        beta_b = sb("beta_b", [P, D])
        zero = sb("zero", [P, D])
        filler = sb("filler", [P, ROW])
        token = sb("token", [P, TG])
        before_sum = sb("before_sum", [P, 2, E], BF16)

        p0 = ExitStack()
        ctx_sb = sb("ctx_sb", [SK, B, D], scope=p0)
        ctxT = sb("ctxT", [P, KC, BK], scope=p0)
        wk_sb = sb("wk_sb", [P, KC, HD], scope=p0)
        wv_sb = sb("wv_sb", [P, KC, HD], scope=p0)
        wo_sb = sb("wo_sb", [P, HP, D], scope=p0)
        NB = 3 * HP + KC
        bias_rows = sb("bias_rows", [NB, P], scope=p0)
        biasT = sb("biasT", [P, NB], scope=p0)
        bo_h = sb("bo_h", [P, KC], scope=p0)
        bq2 = sb("bq2", [P, HP, 2], scope=p0)
        wqT = sb("wqT", [P, HP, D], scope=p0)
        kT = sb("kT", [P, HP, BK], scope=p0)
        vT = sb("vT", [P, HP, BK], scope=p0)
        voT = sb("voT", [P, B, HKP], scope=p0)
        sbias = sb("sbias", [SK, B, 3, NH], BF16, scope=p0)
        sres = sb("sres", [SK, 2, B, NH], scope=p0)
        sbiasT = sb("sbiasT", [3 * NH, B, SK], BF16, scope=p0)
        st1 = sb("st1", [P, NT, 6], scope=p0)
        mv1 = sb("mv1", [P, NT, 2], scope=p0)
        nw1 = sb("nw1", [P, 4, NT], scope=p0)
        p0.close()

        p1 = ExitStack()
        xin = sb("xin", [P, TG, D], scope=p1)
        xn = sb("xn", [P, TG, D], scope=p1)
        xnT = sb("xnT", [P, 2, KC, P], scope=p1)
        sm = sb("sm", [P, 2, HKP], scope=p1)
        smax = sb("smax", [P, 2, NH], scope=p1)
        ssum = sb("ssum", [P, 2, NH], scope=p1)
        sinv = sb("sinv", [P, 2, NH], scope=p1)
        pT = sb("pT", [P, 2, CK, P], scope=p1)
        res = sb("res", [P, TG, D], scope=p1)
        scaled = sb("scaled", [P, TG, D], scope=p1)
        xres = sb("xres", [P, 2, TG, D], scope=p1)
        x2 = sb("x2", [P, 2, TG, D], scope=p1)
        rows = sb("rows", [P, 2, TG, ROW], scope=p1)
        xn2T = sb("xn2T", [P, KC, GT], scope=p1)
        ln1g = sb("ln1g", [P, 2, TG, 2], scope=p1)
        st2 = sb("st2", [P, TG, 6], scope=p1)
        mv2 = sb("mv2", [P, TG, 2], scope=p1)
        nw2 = sb("nw2", [P, 4, TG], scope=p1)
        st3 = sb("st3", [P, TG, 6], scope=p1)
        mv3 = sb("mv3", [P, TG, 2], scope=p1)
        nw3 = sb("nw3", [P, 4, TG], scope=p1)
        nmr3 = sb("nmr3", [P, TG], scope=p1)
        logits = sb("logits", [P, TG, E], scope=p1)
        lmax = sb("lmax", [P, TG], scope=p1)
        lsum = sb("lsum", [P, TG], scope=p1)
        linv = sb("linv", [P, TG], scope=p1)
        lexp = sb("lexp", [P, TG, E], scope=p1)
        prob = sb("prob", [P, TG, E], scope=p1)
        top = sb("top", [P, TG, 8], scope=p1)
        topi = sb("topi", [P, TG, 8], U32, scope=p1)
        topf = sb("topf", [P, TG, TOPK], scope=p1)
        onehot = sb("onehot", [P, TG, TOPK, E], scope=p1)
        mask = sb("mask", [P, TG, E], BF16, scope=p1)
        gsum = sb("gsum", [P, E], scope=p1)
        pos = sb("pos", [P, TG, E], scope=p1)
        valid = sb("valid", [P, TG, E], scope=p1)
        base_e = sb("base_e", [P, TG, E], scope=p1)
        slot_e = sb("slot_e", [P, TG, E], scope=p1)
        wmask = sb("wmask", [P, TG, E], scope=p1)
        picked = sb("picked", [P, TG, TOPK, E], scope=p1)
        slotf = sb("slotf", [P, TG, TOPK], scope=p1)
        slot = sb("slot", [P, 2, TG, TOPK], U32, scope=p1)
        p1.close()

        count = sb("count", [P, E])
        fill_at = sb("fill_at", [P, E], I32)
        nblk_i = sb("nblk_i", [P, 2, E], I32)
        nblk = sb("nblk", [P, E])
        upto = sb("upto", [P, E, E])
        nupto = sb("nupto", [P, E, E])
        blocks_upto = sb("blocks_upto", [P, E])
        past = sb("past", [P, 2, E])
        pastn = sb("pastn", [P, 2, E])
        tabw = sb("tabw", [P, 6, 2])
        tabf = sb("tabf", [P, 2, 3])
        tab = sb("tab", [3, LAG + BLOCKS + NX], I32)
        xg = sb("xg", [P, 2, KC, GT])
        sg = sb("sg", [P, KC, GT])
        sh = sb("sh", [P, KC, GT])
        z_sb = sb("z_sb", [P, TG, D])
        xblk = sb("xblk", [P, NX, ROW])
        xbT = sb("xbT", [P, 2, KC, P])
        eg = sb("eg", [P, 2, H])
        eh = sb("eh", [P, 2, H])
        ehT = sb("ehT", [P, 2, P])
        eo = sb("eo", [P, NACC, D])
        ysum = sb("ysum", [P, 2, NACC, TG, D])

        psum = stack.enter_context(nc.psum_tensor("psum", [P, 8 * BANK], F32))

        def bank(i, n=1):
            return psum[:, i * BANK:(i + n) * BANK]

        scores_ps, pt_ps, o_ps, m_ps = bank(0, 3), bank(3, 3), bank(6), bank(7)

        s = {n: sem(n) for n in """consts_raw consts upto_raw upto_ready
            ld_ctx ld_bias ld_wq ld_wk ld_wv ld_wo ld_bc ld_small ld_xs early_w late_w zeroed dummy_filled
            p0_psum p0_act p0_dve bo_h_ready bq2_ready voT_padded split_step sbias_moved
            ln1_stats ln1_aggr ln1_step ln1_ready ln1g_ready pad_ready
            xn_ready xt_psum xnT_sbuf scores_psum smax_ready shifted exped summed inverted probs_ready
            pt_psum pT_sbuf out_psum res_ready res_stats mv2_ready scaled_ready ln2_step xb_ready x2_ready
            x2_stats mv3_ready ln3_step nmr3_ready rows_ready xn2T_psum xn2T_sbuf xn2T_stored
            logits_psum logits_sbuf lmax_ready lshifted lexped lsum_ready linv_ready prob_ready top_ready topi_ready
            topf_ready onehot_ready mask_ready gsum_ready earlier_ready prefix_psum pos_sbuf valid_ready base_ready
            slot_e_ready picked_ready slotf_ready slot_ready wmask_ready weights_ready tokencol_ready token_ready
            count_psum tab_step fill_ready tab_psum tab_ready filled
            s_psum s_silu s_gated z_psum z_sbuf z_stored
            xbT_psum xbT_sbuf eh_psum eg_ready eh_ready ehT_psum ehT_sbuf eo_psum eo_ready
            ysum_a ysum_b ysum_c""".split()}
        ld_xin = [sem(f"ld_xin{t}") for t in range(TG)]
        ld_xres = [sem(f"ld_xres{p}") for p in range(2)]
        lists_ready = [sem(f"lists_ready{p}") for p in range(2)]
        x2_stored = [sem(f"x2_stored{p}") for p in range(2)]
        ld_xg = [sem(f"ld_xg{p}") for p in range(2)]
        ld_x = [sem(f"ld_xblk{i}") for i in range(NX)]
        added = [sem(f"added{i}") for i in range(NACC)]
        ld_y = [sem(f"ld_y{p}") for p in range(2)]
        stored = [sem(f"stored{p}") for p in range(2)]

        def wait(eng, name, n):
            if not isinstance(n, int) or n > 0:
                eng.wait_ge(s[name] if isinstance(name, str) else name, n)

        def counter(eng, name, first, by):
            due = eng.alloc_register(f"due_{name}")
            eng.reg_mov(due, first)

            def wait_due(n):
                if isinstance(n, int):
                    wait(eng, name, n)
                else:
                    eng.wait_ge(s[name], due)
                    eng.reg_add(due, due, by)
            return wait_due

        def ago(j, p, d):
            return j + (p - d) // 2, (p - d) % 2

        def live(j, p):
            return not isinstance(j, int) or 0 <= 2 * j + p < NG

        def tile_ago(j, p, t, d):
            return (*ago(j, p, -((t - d) // TG)), (t - d) % TG)

        def num(j, p, t=None):
            return j * 2 + p if t is None else j * (2 * TG) + (p * TG + t)

        def wrap(n, size):
            return n if isinstance(n, int) else n % size

        def phase1(eng, step):
            for g in range(2):
                for t in range(TG):
                    step(0, g, t)
            with eng.Fori(1, NG // 2) as j:
                for p in range(2):
                    for t in range(TG):
                        step(j, p, t)
            for g in range(2):
                for t in range(TG):
                    step(NG // 2, g, t)

        def turns(eng, stages, order, load_turn=None):
            def turn(i, qs, skip):
                of_turn = load_turn(i) if load_turn else None
                for q in qs:
                    for lag in order:
                        if not skip(q, lag):
                            stages[lag](i + (q - lag) // NX, (q - lag) % NX, of_turn and of_turn(q, lag))

            turn(0, range(NX), lambda q, lag: q < lag)
            with eng.Fori(1, TURNS) as i:
                turn(i, range(NX), lambda q, lag: False)
            turn(TURNS, range(LAG), lambda q, lag: q >= lag)

        def table(eng, name, row, n, max_val):
            regs = [eng.alloc_register(f"{name}{k}") for k in range(n)]

            def load_turn(i):
                eng.reg_load(regs, tab[row:row + 1, bass.ds(i * NX, n)])
                values = [eng.snap(r, min_val=0, max_val=max_val) for r in regs]
                return lambda q, lag: values[q - lag + LAG] if q - lag + LAG < n else None
            return load_turn

        products = [("bias",)]
        products += [("ctx", b) for b in range(B)]
        products += [("k", j) for j in range(HP)]
        products += [("wq", j) for j in range(HP)]
        products += [("sbias",)]
        products += [("a", d, h) for h in range(NH) for d in range(KC)]
        products += [("sbiasT",)]
        products += [("v", j) for j in range(HP)]
        for d in range(KC):
            products += [("vo", d, h) for h in range(NH)]
            products += [("voT", d, b, c) for b in range(B) for c in range(0, CK, 4)]
        number = {q: i for i, q in enumerate(products)}
        mover = {q: "dve" if i % 2 or q[0][:5] == "sbias" else "act" for i, q in enumerate(products)}
        moved_by = {e: [q for q in products if mover[q] == e] for e in ("act", "dve")}

        def p0_moved(eng, *qs):
            for e in ("act", "dve"):
                last = max((moved_by[e].index(q) for q in qs if mover[q] == e), default=None)
                if last is not None:
                    eng.wait_ge(s["p0_" + e], last + 1)

        def p0_bank(q):
            return bank(number[q] % 8)

        def phase0_over(eng):
            eng.wait_ge(s["ln1_ready"], 1)
            eng.wait_ge(s["sbias_moved"], 16 * 3 * B)
            eng.wait_ge(s["p0_act"], len(moved_by["act"]))
            eng.wait_ge(s["p0_dve"], len(moved_by["dve"]))

        def phase1_over(eng):
            for p in range(2):
                eng.wait_ge(lists_ready[p], 16 * TG * TOPK * NG // 2)
                eng.wait_ge(x2_stored[p], 16 * NG // 2)
            eng.wait_ge(s["xn2T_stored"], 16 * NG)
            eng.wait_ge(s["weights_ready"], NG)
            for t in range(TG):
                eng.wait_ge(ld_xin[t], 16 * (NG + 1))
            eng.wait_ge(s["xn_ready"], NT + 2)
            eng.wait_ge(s["xnT_sbuf"], NT + 1)

        block = stack.enter_context(nc.Block())

        @block.sync
        def _(sp):
            sp.dma_start(ctx_sb[:, :, :], ctx.rearrange("b k d -> k b d")).then_inc(s["ld_ctx"], 16)
            for i, v in enumerate((bq, bk, bv, bo)):
                n = v.shape[0] // P
                sp.dma_start(bias_rows[i * HP:i * HP + n, :], v.rearrange("(c p) -> c p", p=P)
                             ).then_inc(s["ld_bias"], 16)
            for w_sb, w, name in ((wk_sb[:, :, :], Wk, "ld_wk"), (wq_sb, Wq, "ld_wq"), (wv_sb[:, :, :], Wv, "ld_wv")):
                sp.dma_start(w_sb, w.rearrange("(k p) n -> p k n", p=P)).then_inc(s[name], 16)
            sp.dma_start(wo_sb[:, :, :], Wo.rearrange("(c p) n -> p c n", p=P)).then_inc(s["ld_wo"], 16)
            for t_sb, v in ((gamma_b, gamma), (beta_b, beta)):
                sp.dma_start(t_sb[:, :], v.partition_broadcast(P)).then_inc(s["ld_bc"], 16)
            for g in range(NG):
                if g:
                    sp.wait_ge(s["ln1_stats"], g * TG)
                sp.dma_start(xs, xt[g * GT:(g + 1) * GT, :].rearrange("(t p) d -> p t d", p=P)
                             ).then_inc(s["ld_xs"], 16)
            sp.dma_start(wg[:, :, :], Wg.rearrange("(k p) n -> p k n", p=P)).then_inc(s["ld_small"], 16)
            for i, w in enumerate((Ws1, Ws3)):
                sp.dma_start(ws13[:, :, i * HS:(i + 1) * HS], w.rearrange("(k p) n -> p k n", p=P)
                             ).then_inc(s["ld_small"], 16)
            sp.dma_start(ws2[:, :, :], Ws2.rearrange("(k p) n -> p k n", p=P)).then_inc(s["ld_small"], 16)

            sp.wait_ge(s["p0_dve"], moved_by["dve"].index(("sbiasT",)) + 1)
            for i in range(3):
                for b in range(B):
                    sp.dma_start(bias3[i:i + 1, b, :].rearrange("o (h k) -> o h k", h=NH),
                                 sbiasT[i * NH:(i + 1) * NH, b, :]).then_inc(s["sbias_moved"], 16)

            phase0_over(sp)

            def load_x(j, p, t):
                sp.dma_start(xin[:, t, :], xt[bass.ds(wrap(num(j, p, t), NT) * P, P), :]).then_inc(ld_xin[t], 16)

            for t in range(TG):
                load_x(0, 0, t)

            def load_experts(e0, e1, name):
                for k in range(KC):
                    for i, w in enumerate((W1, W3)):
                        at = (2 * k + i) * H
                        sp.dma_start(ew[:, e0:e1, at:at + H], w[e0:e1, k * P:(k + 1) * P, :].rearrange("e p n -> p e n")
                                     ).then_inc(s[name], 16)
                sp.dma_start(ew[:, e0:e1, 2 * D:3 * D], W2[e0:e1].rearrange("e p n -> p e n")).then_inc(s[name], 16)

            load_experts(0, EARLY, "early_w")
            sp.wait_ge(s["consts"], 1)
            for a in acc[2:]:
                sp.dma_start(a.rearrange("(p r) d -> p r d", p=P),
                             zero[:, :].unsqueeze(1).to_broadcast([P, YROWS // P, D])).then_inc(s["zeroed"], 16)
            for a in acc[:2]:
                sp.dma_start(a[T:YROWS, :], zero[:, :]).then_inc(s["zeroed"], 16)
            sp.dma_start(lists[DUMMY:DUMMY + P, :], filler[:, :]).then_inc(s["dummy_filled"], 16)

            def step(j, p, t):
                jn, pn = ago(j, p, -1)
                if live(j, p) and live(jn, pn):
                    wait(sp, "xn_ready", num(j, p, t) + 1)
                    load_x(jn, pn, t)
                if t == 2 and live(j, p):
                    wait(sp, "x2_ready", num(*ago(j, p, 1)) * TG)
                    sp.dma_start(xres[:, p, :, :], xt[bass.ds(num(j, p) * GT, GT), :]
                                 .rearrange("(t p) d -> p t d", p=P)).then_inc(ld_xres[p], 16)
                if t == 3 and live(*ago(j, p, 1)):
                    jh, ph = ago(j, p, 1)
                    wait(sp, "x2_ready", (num(jh, ph) + 1) * TG)
                    sp.dma_start(acc[0][bass.ds(num(jh, ph) * GT, GT), :].rearrange("(t p) d -> p t d", p=P),
                                 x2[:, ph, :, :]).then_inc(x2_stored[ph], 16)
                    wait(sp, "xn2T_sbuf", (num(jh, ph) + 1) * 2)
                    sp.dma_start(xn2T_d[bass.ds(num(jh, ph), 1), :, :].rearrange("o p n -> (o p) n"),
                                 xn2T[:, :, :].rearrange("p k n -> p (k n)")).then_inc(s["xn2T_stored"], 16)

            phase1(sp, step)

            sp.wait_ge(s["scores_psum"], NT)
            sp.wait_ge(s["out_psum"], NT)
            late = E - EARLY
            for e in range(EARLY, E, late // 3):
                load_experts(e, e + late // 3, "late_w")

            def load_xg(g):
                sp.dma_start(xg[:, g % 2, :, :].rearrange("p k n -> p (k n)"), xn2T_d[g]).then_inc(ld_xg[g % 2], 16)

            phase1_over(sp)
            sp.wait_ge(s["xn2T_stored"], 16 * NG)
            load_xg(0)
            load_xg(1)
            sp.wait_ge(s["fill_ready"], 1)
            with sp.Fori(0, E) as e:
                at = sp.value_load(fill_at[0:1, bass.ds(e, 1)], min_val=0, max_val=DUMMY - P)
                sp.dma_start(lists[bass.ds(at, P), :], filler[:, :]).then_inc(s["filled"], 16)
            for g in range(NG):
                sp.wait_ge(s["z_sbuf"], 2 * (g + 1))
                sp.dma_start(acc[1][g * GT:(g + 1) * GT, :].rearrange("(t p) d -> p t d", p=P), z_sb[:, :, :]
                             ).then_inc(s["z_stored"], 16)
                if g + 2 < NG:
                    sp.wait_ge(s["s_psum"], 2 * (g + 1))
                    load_xg(g + 2)

            sp.wait_ge(s["filled"], 16 * E)
            sp.wait_ge(s["dummy_filled"], 16)
            for p in range(2):
                sp.wait_ge(lists_ready[p], 16 * TG * TOPK * NG // 2)
            sp.wait_ge(s["tab_ready"], 1)

            rows_of = table(sp, "first_row", 0, LAG + NX, DUMMY)

            def load_turn(i, of_turn):
                for q in range(NX):
                    if not isinstance(i, int):
                        sp.wait_ge(added[q % NACC], i * (16 * NX // NACC) + 16 * (q // NACC - 1))
                    sp.dma_start(xblk[:, q, :], lists[bass.ds(of_turn(q, 0), P), :]).then_inc(ld_x[q], 16)

            load_turn(0, rows_of(0))
            with sp.Fori(1, TURNS) as i:
                load_turn(i, rows_of(i))

            def load_y(g):
                for a in range(NACC):
                    sp.dma_start(ysum[:, g % 2, a, :, :], acc[a][g * GT:(g + 1) * GT, :]
                                 .rearrange("(t p) d -> p t d", p=P)).then_inc(ld_y[g % 2], 16)

            for q in range(NACC):
                sp.wait_ge(added[q], 16 * BLOCKS // NACC)
            load_y(0)
            load_y(1)
            for g in range(NG):
                sp.wait_ge(s["ysum_c"], g + 1)
                sp.dma_start(ot[g * GT:(g + 1) * GT, :].rearrange("(t p) d -> p t d", p=P), ysum[:, g % 2, 0, :, :]
                             ).then_inc(stored[g % 2], 16)
                if g + 2 < NG:
                    sp.wait_ge(stored[g % 2], 16 * (g // 2 + 1))
                    load_y(g + 2)
            for p in range(2):
                sp.wait_ge(stored[p], 16 * NG // 2)

        @block.gpsimd
        def _(pool):
            kw = dict(allow_small_or_imprecise_dtypes=True)
            raw = [pool.memset(ident[:, :], 0.0),
                   pool.memset(before[:, :], 1.0),
                   pool.memset(onesb[:, :], 1.0),
                   pool.memset(ones3[:, :], 1.0),
                   pool.memset(zero[:, :], 0.0),
                   pool.memset(filler[:, :], 0.0),
                   pool.memset(before_sum[:, :, :], 0.0),
                   pool.iota(iota_e[:, :], [[1, E]], base=0, channel_multiplier=0, **kw),
                   pool.iota(region[:, :], [[REG, E]], base=-TRASH, channel_multiplier=-1, **kw),
                   pool.iota(region0[:, :], [[REG, E]], base=0, channel_multiplier=0, **kw),
                   pool.iota(trash_p[:, :], [[0, 1]], base=TRASH, channel_multiplier=1, **kw),
                   pool.iota(block_i[:, :], [[P, 2]], base=0, channel_multiplier=1, **kw),
                   pool.iota(token[:, :], [[P, TG]], base=0, channel_multiplier=1, **kw)]
            for ins in raw:
                ins.then_inc(s["consts_raw"], 1)
            pool.wait_ge(s["consts_raw"], len(raw))
            pool.iota(filler[:, D:D + 1].bitcast(I32), [[0, 1]], base=T, channel_multiplier=1
                      ).then_inc(s["consts_raw"], 1)
            pool.affine_select(out=ident[:, :], in_=ident[:, :], compare_op=ALU.not_equal, fill=1.0, base=0,
                               pattern=[[-1, P]], channel_multiplier=1).then_inc(s["consts_raw"], 1)
            pool.affine_select(out=before[:, :], in_=before[:, :], compare_op=ALU.is_gt, fill=0.0, base=0,
                               pattern=[[1, P]], channel_multiplier=-1).then_inc(s["consts_raw"], 1)
            pool.wait_ge(s["consts_raw"], len(raw) + 3)
            pool.tensor_copy(identb[:, :], ident[:, :]).then_inc(s["consts"], 1)

            phase0_over(pool)
            pool.wait_ge(s["ld_bc"], 32)
            slots_due = counter(pool, "slot_ready", 1, 1)

            def step(j, p, t):
                if live(j, p):
                    wait(pool, "inverted", num(j, p, t) + 1)
                    e3 = sm[:, t % 2, 0:HK].rearrange("p (h k) -> p h k", h=NH)
                    pool.tensor_tensor(e3, e3, sinv[:, t % 2, :].unsqueeze(2).to_broadcast([P, NH, SK]), ALU.mult
                                       ).then_inc(s["probs_ready"], 1)
                if t == 0 and live(*ago(j, p, 1)):
                    jh, ph = ago(j, p, 1)
                    wait(pool, ld_xres[ph], (jh + 1) * 16)
                    pool.tensor_tensor(xres[:, ph, :, :], xres[:, ph, :, :],
                                       beta_b[:, :].unsqueeze(1).to_broadcast([P, TG, D]), ALU.add
                                       ).then_inc(s["xb_ready"], 1)
                if t >= 2 and live(*ago(j, p, 2)):
                    jh, ph = ago(j, p, 2)
                    if t == 2:
                        wait(pool, "rows_ready", (num(jh, ph) + 1) * TG)
                        wait(pool, "tokencol_ready", num(jh, ph) + 1)
                        wait(pool, "weights_ready", num(jh, ph) + 1)
                        slots_due(num(jh, ph) + 1)
                    for tt in ((0, 1) if t == 2 else (2, 3)):
                        for k in range(TOPK):
                            pool.indirect_dma_start(
                                out=lists, out_offset=bass.IndirectOffsetOnAxis(ap=slot[:, ph, tt, k:k + 1], axis=0),
                                in_=rows[:, ph, tt, :], in_offset=None).then_inc(lists_ready[ph], 16)

            phase1(pool, step)

            phase1_over(pool)
            pool.memset(upto[:, :, :], 1.0).then_inc(s["upto_raw"], 1)
            pool.wait_ge(s["upto_raw"], 1)
            pool.affine_select(out=upto[:, :, :], in_=upto[:, :, :], compare_op=ALU.is_ge, fill=0.0, base=0,
                               pattern=[[1, E], [-1, E]], channel_multiplier=0).then_inc(s["upto_ready"], 1)

            pool.wait_ge(s["zeroed"], 16 * NACC)
            pool.wait_ge(s["z_stored"], 16 * NG)

            outputs_due = counter(pool, "eo_ready", NX + 1, 1)

            def add_block(i, q):
                a = q % NACC
                if q >= NACC or not isinstance(i, int):
                    pool.wait_ge(added[a], i * (16 * NX // NACC) + 16 * (q // NACC))
                outputs_due(i * NX + (q + 1))
                pool.indirect_dma_start(
                    out=acc[a], out_offset=bass.IndirectOffsetOnAxis(ap=xblk[:, q, D:D + 1].bitcast(U32), axis=0),
                    in_=eo[:, a, :], in_offset=None, compute_op=ALU.add).then_inc(added[a], 16)

            for q in range(NX):
                add_block(0, q)
            with pool.Fori(1, TURNS) as i:
                for q in range(NX):
                    add_block(i, q)

            for g in range(NG):
                pool.wait_ge(ld_y[g % 2], 16 * NACC * (g // 2 + 1))
                y = ysum[:, g % 2, :, :, :]
                pool.tensor_tensor(y[:, 2], y[:, 2], y[:, 3], ALU.add).then_inc(s["ysum_a"], 1)

        def p0_copy(eng, dst, src, bias=None):
            if eng == "act":
                if bias is None:
                    return nc.scalar.activation(dst, src, ACT.Copy)
                return nc.scalar.activation(dst, src, ACT.Identity, bias=bias)
            if bias is None:
                return nc.vector.tensor_copy(dst, src)
            return nc.vector.tensor_scalar(dst, src, bias, None, ALU.add)

        def p0_move(e, q):
            src, kind = p0_bank(q), q[0]
            if kind == "bias":
                return p0_copy(e, biasT[:, :], src[:, 0:NB])
            if kind == "ctx":
                return p0_copy(e, ctxT[:, :, q[1] * SK:(q[1] + 1) * SK],
                               src[:, 0:KC * SK].rearrange("p (k n) -> p k n", k=KC))
            if kind == "wq":
                return p0_copy(e, wqT[:, q[1], :], src[:, 0:D])
            if kind == "k":
                return p0_copy(e, kT[:, q[1], :], src[:, 0:BK], biasT[:, HP + q[1]:HP + q[1] + 1])
            if kind == "v":
                return p0_copy(e, vT[:, q[1], :], src[:, 0:BK], biasT[:, 2 * HP + q[1]:2 * HP + q[1] + 1])
            if kind == "a":
                return p0_copy(e, A[:, q[1], :, q[2] * SK:(q[2] + 1) * SK],
                               src[:, 0:BK].rearrange("p (b n) -> p b n", b=B))
            if kind == "vo":
                return p0_copy(e, voT[:, :, q[2] * SK:(q[2] + 1) * SK],
                               src[:, 0:BK].rearrange("p (b n) -> p b n", b=B), bo_h[:, q[1]:q[1] + 1])
            if kind == "voT":
                _, d, b, c = q
                n = min(4, CK - c)
                return p0_copy(e, VO[:, b, c:c + n, d * P:(d + 1) * P],
                               src[:, 0:n * P].rearrange("p (c n) -> p c n", c=n))
            if kind == "sbiasT":
                return p0_copy(e, sbiasT[:, :, :], src.bitcast(BF16)[0:3 * NH, 0:B * SKE]
                               .rearrange("p (b k) -> p b k", b=B)[:, :, 0:SK])
            raise AssertionError(q)

        @block.scalar
        def _(act):
            for q in moved_by["act"]:
                act.wait_ge(s["p0_psum"], number[q] + 1)
                if q[0] in ("k", "v"):
                    p0_moved(act, ("bias",))
                if q[0] == "vo":
                    act.wait_ge(s["bo_h_ready"], 1)
                p0_move("act", q).then_inc(s["p0_act"], 1)

            def norm_x(j, p, t):
                wait(act, "ln1g_ready", num(j, p) + 1)
                wait(act, "res_ready", num(j, p, t) + (1 - TG))
                wait(act, ld_xin[t], (num(j, p) + 1) * 16)
                nc.scalar.activation(xn[:, t, :], xin[:, t, :], ACT.Identity, scale=ln1g[:, p, t, 0:1],
                                     bias=ln1g[:, p, t, 1:2]).then_inc(s["xn_ready"], 1)

            def move_xnT(j, p, t):
                wait(act, "scores_psum", num(j, p, t) - 1)
                wait(act, "xt_psum", num(j, p, t) + 1)
                nc.scalar.activation(xnT[:, t % 2, :, :].rearrange("p k n -> p (k n)"), pt_ps[:, HKP:HKP + D], ACT.Copy
                                     ).then_inc(s["xnT_sbuf"], 1)

            def move_xn2T(jh, ph, half):
                g = num(jh, ph)
                wait(act, "xn2T_stored", g * 16)
                wait(act, "xn2T_psum", g * 2 + (half + 1))
                nc.scalar.activation(xn2T[:, :, half * 2 * P:(half + 1) * 2 * P],
                                     m_ps.rearrange("p (k n) -> p k n", k=KC), ACT.Copy).then_inc(s["xn2T_sbuf"], 1)

            phase0_over(act)
            norm_x(0, 0, 0)
            norm_x(0, 0, 1)
            move_xnT(0, 0, 0)

            def step(j, p, t):
                jh, ph = ago(j, p, 1)
                if t == 3 and live(jh, ph):
                    move_xn2T(jh, ph, 0)
                j2, p2 = ago(j, p, 2)
                if t == 1 and live(j2, p2):
                    wait(act, "slot_e_ready", num(j2, p2))
                    wait(act, "prefix_psum", num(j2, p2) + 1)
                    nc.scalar.activation(pos[:, :, :].rearrange("p t e -> p (t e)"), m_ps[:, 0:TG * E], ACT.Copy
                                         ).then_inc(s["pos_sbuf"], 1)
                jm, pm, tm = tile_ago(j, p, t, 1)
                if live(jm, pm):
                    m = num(jm, pm, tm)
                    for c in range(0, CK, 4):
                        wait(act, "out_psum", m - 1)
                        if c < 8:
                            wait(act, "pt_psum", m * 2 + (c // 4 + 1))
                        else:
                            wait(act, "xt_psum", m + 3)
                        k = min(4, CK - c)
                        nc.scalar.activation(pT[:, tm % 2, c:c + k, :].rearrange("p c n -> p (c n)"),
                                             pt_ps[:, c * P:(c + k) * P], ACT.Copy).then_inc(s["pT_sbuf"], 1)
                jn, pn, tn = tile_ago(j, p, t, -1)
                if live(j, p):
                    if live(jn, pn):
                        move_xnT(jn, pn, tn)
                    wait(act, "shifted", num(j, p, t) + 1)
                    nc.scalar.activation(sm[:, t % 2, 0:HK], sm[:, t % 2, 0:HK], ACT.Exp).then_inc(s["exped"], 1)
                if t == 3 and live(jh, ph):
                    move_xn2T(jh, ph, 1)
                    wait(act, "lshifted", num(jh, ph))
                    wait(act, "logits_psum", num(jh, ph) + 1)
                    nc.scalar.activation(logits[:, :, :].rearrange("p t e -> p (t e)"), m_ps[:, 0:TG * E], ACT.Copy
                                         ).then_inc(s["logits_sbuf"], 1)
                jx, px, tx = tile_ago(j, p, t, -2)
                if live(jx, px):
                    norm_x(jx, px, tx)
                if t == 2 and live(jh, ph):
                    for tt in range(TG):
                        wait(act, lists_ready[ph], jh * (16 * TG * TOPK))
                        wait(act, "nmr3_ready", num(jh, ph) + 1)
                        nc.scalar.activation(rows[:, ph, tt, 0:D], x2[:, ph, tt, :], ACT.Identity,
                                             scale=nw3[:, 2, tt:tt + 1], bias=nmr3[:, tt:tt + 1]
                                             ).then_inc(s["rows_ready"], 1)
                if t == 0 and live(j2, p2):
                    wait(act, "lshifted", num(j2, p2) + 1)
                    nc.scalar.activation(lexp[:, :, :], lexp[:, :, :], ACT.Exp).then_inc(s["lexped"], 1)

            phase1(act, step)

            phase1_over(act)
            def z_out(g):
                for half in range(2):
                    act.wait_ge(s["z_psum"], 2 * g + half + 1)
                    if g:
                        act.wait_ge(s["z_stored"], 16 * g)
                    nc.scalar.activation(z_sb[:, 2 * half:2 * half + 2, :].rearrange("p t d -> p (t d)"),
                                         bank(4 + half), ACT.Copy).then_inc(s["z_sbuf"], 1)

            for g in range(NG):
                for c in range(KC):
                    act.wait_ge(s["s_psum"], 2 * g + c + 1)
                    if g:
                        act.wait_ge(s["s_gated"], 2 * (g - 1) + c + 1)
                    nc.scalar.activation(sg[:, c, :], bank(c), ACT.Silu).then_inc(s["s_silu"], 1)
                    if c == 0 and g:
                        z_out(g - 1)
            z_out(NG - 1)

            def silu(i, q, _):
                b = i * NX + q
                wait(act, "eh_ready", b - 1)
                wait(act, "eh_psum", b + 1)
                nc.scalar.activation(eg[:, q % 2, :], bank(2 + q % 2)[:, 0:H], ACT.Silu).then_inc(s["eg_ready"], 1)

            act.wait_ge(s["tab_ready"], 1)
            outs_due = counter(act, "eo_psum", NX - LAG + 1, 1)

            def weigh(i, q, col):
                a = q % NACC
                if q >= NACC or not isinstance(i, int):
                    act.wait_ge(added[a], i * (16 * NX // NACC) + 16 * (q // NACC))
                outs_due(i * NX + (q + 1))
                nc.scalar.activation(eo[:, a, :], bank(6 + q % 2)[:, 0:D], ACT.Copy, scale=xblk[:, q, bass.ds(col, 1)]
                                     ).then_inc(s["eo_ready"], 1)

            turns(act, {1: silu, LAG: weigh}, (1, LAG), table(act, "weight_col", 2, NX, ROW - 1))

        def rsqrt(dve, name, base, var, eps, w):
            def after(i):
                dve.wait_ge(s[name], base + i)

            nc.vector.tensor_scalar(w[:, 0, :], var, eps, None, ALU.add).then_inc(s[name], 1)
            after(1)
            nc.vector.tensor_scalar(w[:, 1, :].bitcast(I32), w[:, 0, :].bitcast(I32), 1, None, ALU.logical_shift_right
                                    ).then_inc(s[name], 1)
            after(2)
            nc.vector.tensor_scalar(w[:, 2, :].bitcast(I32), w[:, 1, :].bitcast(I32), -1.0, float(RSQRT_SEED),
                                    ALU.mult, ALU.add).then_inc(s[name], 1)
            for k in range(NEWTON):
                after(3 + 3 * k)
                nc.vector.tensor_tensor(w[:, 3, :], w[:, 2, :], w[:, 2, :], ALU.mult).then_inc(s[name], 1)
                after(4 + 3 * k)
                nc.vector.scalar_tensor_tensor(w[:, 1, :], w[:, 3, :], -0.5, w[:, 0, :], ALU.mult, ALU.mult
                                               ).then_inc(s[name], 1)
                after(5 + 3 * k)
                nc.vector.scalar_tensor_tensor(w[:, 2, :], w[:, 1, :], 1.5, w[:, 2, :], ALU.add, ALU.mult
                                               ).then_inc(s[name], 1)

        @block.vector
        def _(dve):
            def stats1(g):
                dve.wait_ge(s["ld_xs"], 16 * (g + 1))
                for t in range(g * TG, (g + 1) * TG):
                    nc.vector.bn_stats(st1[:, t, :], xs[:, t % TG, :]).then_inc(s["ln1_stats"], 1)
                for t in range(g * TG, (g + 1) * TG):
                    dve.wait_ge(s["ln1_stats"], t + 1)
                    nc.vector.bn_aggr(mv1[:, t, :], st1[:, t, :]).then_inc(s["ln1_aggr"], 1)

            def split_bias(q):
                src = p0_bank(q)[0:SK, 0:B * NH].rearrange("k (b h) -> k b h", b=B)
                steps = [lambda: nc.vector.tensor_copy(sbias[:, :, 0, :], src),
                         lambda: nc.vector.tensor_tensor(sres[:, 0], src, sbias[:, :, 0, :], ALU.subtract),
                         lambda: nc.vector.tensor_copy(sbias[:, :, 1, :], sres[:, 0]),
                         lambda: nc.vector.tensor_tensor(sres[:, 1], sres[:, 0], sbias[:, :, 1, :], ALU.subtract),
                         lambda: nc.vector.tensor_copy(sbias[:, :, 2, :], sres[:, 1])]
                for i, step in enumerate(steps):
                    if i:
                        dve.wait_ge(s["split_step"], i)
                    ins = step()
                    ins.then_inc(s["split_step"] if i < len(steps) - 1 else s["p0_dve"], 1)

            nc.vector.memset(bq2[:, :, :], 0.0).then_inc(s["bq2_ready"], 1)
            nc.vector.memset(voT[:, :, HK:HKP], 0.0).then_inc(s["voT_padded"], 1)
            stats_at = {("a", 1, h): g for g, h in enumerate(range(1, NH, 2))}
            for q in products:
                if q[0] == "ctx" and q[1] == B - 1:
                    p0_moved(dve, ("bias",))
                    dve.wait_ge(s["bq2_ready"], 1)
                    for i in range(2):
                        half = slice(i * DH, (i + 1) * DH)
                        nc.vector.tensor_copy(bq2[half, :, i], biasT[half, 0:HP]).then_inc(s["bq2_ready"], 1)
                    nc.vector.tensor_scalar(bo_h[:, :], biasT[:, 3 * HP:NB], 1.0 / NH, None, ALU.mult
                                            ).then_inc(s["bo_h_ready"], 1)
                if mover[q] == "dve":
                    dve.wait_ge(s["p0_psum"], number[q] + 1)
                    if q[0] in ("k", "v"):
                        p0_moved(dve, ("bias",))
                    if q[0] == "vo":
                        dve.wait_ge(s["bo_h_ready"], 1)
                    if q[0] == "sbias":
                        split_bias(q)
                    else:
                        p0_move("dve", q).then_inc(s["p0_dve"], 1)
                if q in stats_at:
                    stats1(stats_at[q])
            dve.wait_ge(s["ln1_aggr"], NT)
            rsqrt(dve, "ln1_step", 0, mv1[:, :, 1], EPS_LN, nw1)
            dve.wait_ge(s["ln1_step"], RSQRT_OPS)
            nc.vector.tensor_copy(ln1[:, :, 0], nw1[:, 2, :]).then_inc(s["ln1_step"], 1)
            dve.wait_ge(s["ln1_step"], RSQRT_OPS + 1)
            nc.vector.scalar_tensor_tensor(ln1[:, :, 1], mv1[:, :, 0], -1.0, nw1[:, 2, :], ALU.mult, ALU.mult
                                           ).then_inc(s["ln1_ready"], 1)

            phase0_over(dve)
            nc.vector.memset(sm[:, :, HK:HKP], 0.0).then_inc(s["pad_ready"], 1)

            res_stats_due = counter(dve, "res_stats", 2 * TG, TG)
            x2_stats_due = counter(dve, "x2_stats", 2 * TG, TG)
            probs_due = counter(dve, "prob_ready", 1, 1)
            tops_due = counter(dve, "top_ready", TG, TG)

            def group_ln1(j, p):
                wait(dve, "xn_ready", (num(j, p) - 1) * TG)
                nc.vector.tensor_scalar(ln1g[:, p, :, :], ln1[:, bass.ds(wrap(num(j, p), NG) * TG, TG), :], 1.0, None, ALU.mult
                                        ).then_inc(s["ln1g_ready"], 1)

            group_ln1(0, 0)

            def second_norm(jh, ph):
                g = num(jh, ph)
                res_stats_due((g + 1) * TG)
                for t in range(TG):
                    nc.vector.bn_aggr(mv2[:, t, :], st2[:, t, :]).then_inc(s["mv2_ready"], 1)
                for t in range(TG):
                    wait(dve, "mv2_ready", g * TG + (t + 1))
                    wait(dve, "x2_ready", (g - 1) * TG + (t + 1))
                    nc.vector.scalar_tensor_tensor(scaled[:, t, :], res[:, t, :], mv2[:, t, 0:1], gamma_b[:, :],
                                                   ALU.subtract, ALU.mult).then_inc(s["scaled_ready"], 1)
                rsqrt(dve, "ln2_step", g * RSQRT_OPS, mv2[:, :, 1], EPS_ATT, nw2)

            def third_norm(jh, ph):
                g = num(jh, ph)
                wait(dve, "xb_ready", g + 1)
                wait(dve, "ln2_step", (g + 1) * RSQRT_OPS)
                for t in range(TG):
                    wait(dve, "scaled_ready", g * TG + (t + 1))
                    wait(dve, x2_stored[ph], jh * 16)
                    wait(dve, "rows_ready", (g - 1) * TG)
                    nc.vector.scalar_tensor_tensor(x2[:, ph, t, :], scaled[:, t, :], nw2[:, 2, t:t + 1],
                                                   xres[:, ph, t, :], ALU.mult, ALU.add).then_inc(s["x2_ready"], 1)
                for t in range(TG):
                    wait(dve, "x2_ready", g * TG + (t + 1))
                    nc.vector.bn_stats(st3[:, t, :], x2[:, ph, t, :]).then_inc(s["x2_stats"], 1)
                x2_stats_due((g + 1) * TG)
                for t in range(TG):
                    nc.vector.bn_aggr(mv3[:, t, :], st3[:, t, :]).then_inc(s["mv3_ready"], 1)
                wait(dve, "rows_ready", g * TG)
                wait(dve, "mv3_ready", (g + 1) * TG)
                rsqrt(dve, "ln3_step", g * RSQRT_OPS, mv3[:, :, 1], EPS_LN, nw3)
                wait(dve, "ln3_step", (g + 1) * RSQRT_OPS)
                nc.vector.scalar_tensor_tensor(nmr3[:, :], mv3[:, :, 0], -1.0, nw3[:, 2, :], ALU.mult, ALU.mult
                                               ).then_inc(s["nmr3_ready"], 1)

            def choose(jh, ph):
                g = num(jh, ph)

                def over_e(a):
                    return a.unsqueeze(2).to_broadcast([P, TG, E])

                wait(dve, "logits_sbuf", g + 1)
                nc.vector.tensor_reduce(lmax[:, :], logits[:, :, :], AX, ALU.max).then_inc(s["lmax_ready"], 1)
                wait(dve, "lmax_ready", g + 1)
                nc.vector.tensor_tensor(lexp[:, :, :], logits[:, :, :], over_e(lmax[:, :]), ALU.subtract
                                        ).then_inc(s["lshifted"], 1)
                wait(dve, "lexped", g + 1)
                nc.vector.tensor_reduce(lsum[:, :], lexp[:, :, :], AX, ALU.add).then_inc(s["lsum_ready"], 1)
                wait(dve, "lsum_ready", g + 1)
                nc.vector.reciprocal(linv[:, :], lsum[:, :]).then_inc(s["linv_ready"], 1)
                wait(dve, "linv_ready", g + 1)
                nc.vector.tensor_tensor(prob[:, :, :], lexp[:, :, :], over_e(linv[:, :]), ALU.mult
                                        ).then_inc(s["prob_ready"], 1)
                probs_due(g + 1)
                for t in range(TG):
                    nc.vector.max(top[:, t, :], prob[:, t, :]).then_inc(s["top_ready"], 1)
                tops_due((g + 1) * TG)
                for t in range(TG):
                    nc.vector.max_index(topi[:, t, :], top[:, t, :], prob[:, t, :]).then_inc(s["topi_ready"], 1)
                wait(dve, "topi_ready", (g + 1) * TG)
                nc.vector.tensor_copy(topf[:, :, :], topi[:, :, 0:TOPK]).then_inc(s["topf_ready"], 1)
                wait(dve, "topf_ready", g + 1)
                nc.vector.tensor_tensor(onehot[:, :, :, :].rearrange("p t k e -> p (t k) e"),
                                        iota_e[:, :].unsqueeze(1).to_broadcast([P, TG * TOPK, E]),
                                        topf[:, :, :].rearrange("p t k -> p (t k)").unsqueeze(2)
                                        .to_broadcast([P, TG * TOPK, E]), ALU.is_equal).then_inc(s["onehot_ready"], 1)
                wait(dve, "onehot_ready", g + 1)
                with nc.allow_low_precision(reason="sums of at most one 1"):
                    nc.vector.tensor_reduce(mask[:, :, :], onehot[:, :, :, :].rearrange("p t k e -> p t e k"), AX,
                                            ALU.add).then_inc(s["mask_ready"], 1)
                wait(dve, "mask_ready", g + 1)
                nc.vector.tensor_reduce(gsum[:, :], mask[:, :, :].rearrange("p t e -> p e t"), AX, ALU.add
                                        ).then_inc(s["gsum_ready"], 1)
                wait(dve, "prefix_psum", g)
                wait(dve, "gsum_ready", g + 1)
                nc.vector.tensor_tensor(before_sum[:, 1 - ph, :], before_sum[:, ph, :], gsum[:, :], ALU.add
                                        ).then_inc(s["earlier_ready"], 1)

            def place(jh, ph):
                g = num(jh, ph)
                wait(dve, "pos_sbuf", g + 1)
                nc.vector.tensor_scalar(valid[:, :, :], pos[:, :, :], float(CAP), None, ALU.is_lt
                                        ).then_inc(s["valid_ready"], 1)
                nc.vector.tensor_tensor(base_e[:, :, :], pos[:, :, :],
                                        region[:, :].unsqueeze(1).to_broadcast([P, TG, E]), ALU.add
                                        ).then_inc(s["base_ready"], 1)
                nc.vector.tensor_tensor(wmask[:, :, :], prob[:, :, :], mask[:, :, :], ALU.mult
                                        ).then_inc(s["wmask_ready"], 1)
                wait(dve, "base_ready", g + 1)
                nc.vector.tensor_tensor(slot_e[:, :, :], base_e[:, :, :], valid[:, :, :], ALU.mult
                                        ).then_inc(s["slot_e_ready"], 1)
                wait(dve, lists_ready[ph], jh * (16 * TG * TOPK))
                wait(dve, "wmask_ready", g + 1)
                nc.vector.tensor_tensor(rows[:, ph, :, D + 1:ROW], wmask[:, :, :], valid[:, :, :], ALU.mult
                                        ).then_inc(s["weights_ready"], 1)
                wait(dve, "slot_e_ready", g + 1)
                nc.vector.tensor_tensor(picked[:, :, :, :], onehot[:, :, :, :],
                                        slot_e[:, :, :].unsqueeze(2).to_broadcast([P, TG, TOPK, E]), ALU.mult
                                        ).then_inc(s["picked_ready"], 1)
                wait(dve, "token_ready", g)
                nc.vector.tensor_copy(rows[:, ph, :, D:D + 1].bitcast(U32), token[:, :].unsqueeze(2)
                                      ).then_inc(s["tokencol_ready"], 1)
                wait(dve, "picked_ready", g + 1)
                nc.vector.tensor_reduce(slotf[:, :, :], picked[:, :, :, :], AX, ALU.add).then_inc(s["slotf_ready"], 1)
                wait(dve, "tokencol_ready", g + 1)
                nc.vector.tensor_scalar(token[:, :], token[:, :], float(GT), None, ALU.add).then_inc(s["token_ready"], 1)
                wait(dve, "slotf_ready", g + 1)
                nc.vector.tensor_scalar(slot[:, ph, :, :], slotf[:, :, :], trash_p[:, 0:1], None, ALU.add
                                        ).then_inc(s["slot_ready"], 1)

            def step(j, p, t):
                n = num(j, p, t)
                heads = "p (h k) -> p h k"
                if live(j, p):
                    wait(dve, "scores_psum", n + 1)
                    sc = scores_ps[:, 0:HK].rearrange(heads, h=NH)
                    nc.vector.tensor_reduce(smax[:, t % 2, :], sc, AX, ALU.max).then_inc(s["smax_ready"], 1)
                    wait(dve, "xt_psum", n + 1 if not isinstance(n, int) or n > 1 else 0)
                    wait(dve, "smax_ready", n + 1)
                    nc.vector.tensor_tensor(sm[:, t % 2, 0:HK].rearrange(heads, h=NH), sc,
                                            smax[:, t % 2, :].unsqueeze(2).to_broadcast([P, NH, SK]), ALU.subtract
                                            ).then_inc(s["shifted"], 1)
                jm, pm, tm = tile_ago(j, p, t, 2)
                if live(jm, pm):
                    m = num(jm, pm, tm)
                    wait(dve, "scaled_ready", m + 1 - TG)
                    wait(dve, "out_psum", m + 1)
                    nc.vector.tensor_tensor(res[:, tm, :], o_ps[:, 0:D], xn[:, tm, :], ALU.add
                                            ).then_inc(s["res_ready"], 1)
                    wait(dve, "res_ready", m + 1)
                    nc.vector.bn_stats(st2[:, tm, :], res[:, tm, :]).then_inc(s["res_stats"], 1)
                if t == 1 and live(*ago(j, p, -1)) and live(j, p):
                    group_ln1(*ago(j, p, -1))
                if live(j, p):
                    wait(dve, "exped", n + 1)
                    nc.vector.tensor_reduce(ssum[:, t % 2, :], sm[:, t % 2, 0:HK].rearrange(heads, h=NH), AX, ALU.add
                                            ).then_inc(s["summed"], 1)
                    wait(dve, "probs_ready", n - 1)
                    wait(dve, "summed", n + 1)
                    nc.vector.reciprocal(sinv[:, t % 2, :], ssum[:, t % 2, :]).then_inc(s["inverted"], 1)
                if t == 0 and live(*ago(j, p, 2)):
                    choose(*ago(j, p, 2))
                if t == 1 and live(*ago(j, p, 2)):
                    place(*ago(j, p, 2))
                if t == 1 and live(*ago(j, p, 1)):
                    second_norm(*ago(j, p, 1))
                if t == 2 and live(*ago(j, p, 1)):
                    third_norm(*ago(j, p, 1))

            phase1(dve, step)

            phase1_over(dve)
            tab_ops = [0]

            def tab_op(ins):
                ins.then_inc(s["tab_step"], 1)
                tab_ops[0] += 1
                dve.wait_ge(s["tab_step"], tab_ops[0])

            tab_op(nc.vector.memset(tab[:, :], 0))
            dve.wait_ge(s["count_psum"], 1)
            tab_op(nc.vector.tensor_scalar(count[:, :], m_ps[:, 0:E], float(CAP), None, ALU.min))
            nc.vector.tensor_tensor(fill_at[:, :], count[:, :], region0[:, :], ALU.add).then_inc(s["fill_ready"], 1)
            tab_op(nc.vector.tensor_scalar(nblk_i[:, 0, :], count[:, :], float(P - 1), None, ALU.add))
            tab_op(nc.vector.tensor_scalar(nblk_i[:, 1, :], nblk_i[:, 0, :], P.bit_length() - 1, None,
                                           ALU.logical_shift_right))
            tab_op(nc.vector.tensor_copy(nblk[:, :], nblk_i[:, 1, :]))
            dve.wait_ge(s["upto_ready"], 1)
            tab_op(nc.vector.tensor_tensor(nupto[:, :, :], upto[:, :, :],
                                           nblk[:, :].unsqueeze(1).to_broadcast([P, E, E]), ALU.mult))
            tab_op(nc.vector.tensor_reduce(blocks_upto[:, :], nupto[:, :, :], AX, ALU.add))
            tab_op(nc.vector.tensor_tensor(past[:, :, :], blocks_upto[:, :].unsqueeze(1).to_broadcast([P, 2, E]),
                                           block_i[:, :].unsqueeze(2).to_broadcast([P, 2, E]), ALU.is_le))
            tab_op(nc.vector.tensor_tensor(pastn[:, :, :], past[:, :, :],
                                           nblk[:, :].unsqueeze(1).to_broadcast([P, 2, E]), ALU.mult))
            expert, first, at, row, row1, row2 = (tabw[:, i, :] for i in range(6))
            tab_op(nc.vector.tensor_reduce(expert, past[:, :, :], AX, ALU.add))
            tab_op(nc.vector.tensor_reduce(first, pastn[:, :, :], AX, ALU.add))
            tab_op(nc.vector.tensor_tensor(at, block_i[:, :], first, ALU.subtract))
            tab_op(nc.vector.tensor_scalar(row, expert, float(REG), None, ALU.mult))
            tab_op(nc.vector.scalar_tensor_tensor(row1, at, float(P), row, ALU.mult, ALU.add))
            tab_op(nc.vector.tensor_scalar(tabf[:, :, 0], row1, float(DUMMY), None, ALU.min))
            tab_op(nc.vector.tensor_scalar(tabf[:, :, 1], expert, float(E - 1), None, ALU.min))
            tab_op(nc.vector.tensor_scalar(tabf[:, :, 2], tabf[:, :, 1], float(D + 1), None, ALU.add))
            dve.wait_ge(s["tab_psum"], 1)
            nc.vector.tensor_copy(tab[:, LAG:LAG + BLOCKS], o_ps[0:3, 0:BLOCKS]).then_inc(s["tab_ready"], 1)

            for g in range(NG):
                for c in range(KC):
                    dve.wait_ge(s["s_silu"], 2 * g + c + 1)
                    if g:
                        dve.wait_ge(s["z_psum"], 2 * g)
                    nc.vector.tensor_tensor(sh[:, c, :], sg[:, c, :], bank(2 + c), ALU.mult).then_inc(s["s_gated"], 1)

            def move_xbT(i, q, _):
                b = i * NX + q
                wait(dve, "eh_psum", b - 1)
                wait(dve, "xbT_psum", b + 1)
                nc.vector.tensor_copy(xbT[:, q % 2, :, :].rearrange("p k n -> p (k n)"), bank(q % 2)[:, 0:D]
                                      ).then_inc(s["xbT_sbuf"], 1)

            def gate(i, q, _):
                b = i * NX + q
                wait(dve, "ehT_psum", b - 1)
                wait(dve, "eg_ready", b + 1)
                nc.vector.tensor_tensor(eh[:, q % 2, :], eg[:, q % 2, :], bank(2 + q % 2)[:, H:2 * H], ALU.mult
                                        ).then_inc(s["eh_ready"], 1)

            def move_ehT(i, q, _):
                b = i * NX + q
                wait(dve, "eo_psum", b - 1)
                wait(dve, "ehT_psum", b + 1)
                nc.vector.tensor_copy(ehT[:, q % 2, :], bank(4 + q % 2)[:, 0:P]).then_inc(s["ehT_sbuf"], 1)

            turns(dve, {0: move_xbT, 1: gate, 2: move_ehT}, (0, 1, 2))

            for g in range(NG):
                y = ysum[:, g % 2, :, :, :]
                dve.wait_ge(ld_y[g % 2], 16 * NACC * (g // 2 + 1))
                nc.vector.tensor_tensor(y[:, 0], y[:, 0], y[:, 1], ALU.add).then_inc(s["ysum_b"], 1)
                dve.wait_ge(s["ysum_a"], g + 1)
                dve.wait_ge(s["ysum_b"], g + 1)
                nc.vector.tensor_tensor(y[:, 0], y[:, 0], y[:, 2], ALU.add).then_inc(s["ysum_c"], 1)

        @block.tensor
        def _(pe):
            mm = nc.tensor.matmul

            def transpose(out, in_):
                n = in_.shape[0]
                return nc.tensor.transpose(out, in_, ident[0:n, 0:n])

            def product(q):
                ps, kind = p0_bank(q), q[0]
                if kind == "bias":
                    pe.wait_ge(s["ld_bias"], 64)
                    return transpose(ps[:, 0:NB], bias_rows[:, :])
                if kind == "ctx":
                    pe.wait_ge(s["ld_ctx"], 16)
                    for k in range(KC):
                        last = transpose(ps[:, k * SK:(k + 1) * SK], ctx_sb[:, q[1], k * P:(k + 1) * P])
                    return last
                if kind == "wq":
                    pe.wait_ge(s["ld_wq"], 16)
                    for k in range(KC):
                        last = transpose(ps[:, k * P:(k + 1) * P], wq_sb[:, k, q[1] * P:(q[1] + 1) * P])
                    return last
                if kind in "kv":
                    w_sb = wk_sb if kind == "k" else wv_sb
                    pe.wait_ge(s["ld_w" + kind], 16)
                    p0_moved(pe, *[("ctx", b) for b in range(B)])
                    for k in range(KC):
                        last = mm(ps[:, 0:BK], w_sb[:, k, q[1] * P:(q[1] + 1) * P], ctxT[:, k, :], start=k == 0,
                                  stop=k == KC - 1)
                    return last
                if kind == "sbias":
                    pe.wait_ge(s["bq2_ready"], 3)
                    p0_moved(pe, *[("k", j) for j in range(HP)])
                    for b in range(B):
                        for j in range(HP):
                            last = mm(ps[0:SK, b * NH + 2 * j:b * NH + 2 * j + 2], kT[:, j, b * SK:(b + 1) * SK],
                                      bq2[:, j, :], start=True, stop=True)
                    return last
                if kind == "sbiasT":
                    p0_moved(pe, ("sbias",))
                    for b in range(B):
                        last = nc.tensor.transpose(ps.bitcast(BF16)[0:3 * NH, b * SKE:b * SKE + SK],
                                                   sbias[:, b, :, :].rearrange("k i h -> k (i h)"), identb[0:SK, 0:SK])
                    return last
                if kind == "a":
                    _, d, h = q
                    half = slice(h % 2 * DH, (h % 2 + 1) * DH)
                    p0_moved(pe, ("wq", h // 2), ("k", h // 2))
                    return mm(ps[:, 0:BK], wqT[half, h // 2, d * P:(d + 1) * P], kT[half, h // 2, :], start=True,
                              stop=True)
                if kind == "vo":
                    _, d, h = q
                    half = slice(h % 2 * DH, (h % 2 + 1) * DH)
                    pe.wait_ge(s["ld_wo"], 16)
                    p0_moved(pe, ("v", h // 2))
                    return mm(ps[:, 0:BK], wo_sb[half, h // 2, d * P:(d + 1) * P], vT[half, h // 2, :], start=True,
                              stop=True)
                _, d, b, c = q
                pe.wait_ge(s["voT_padded"], 1)
                p0_moved(pe, *[("vo", d, h) for h in range(NH)])
                for i in range(min(4, CK - c)):
                    last = transpose(ps[:, i * P:(i + 1) * P], voT[:, b, (c + i) * P:(c + i + 1) * P])
                return last

            pe.wait_ge(s["consts"], 1)
            for i, q in enumerate(products):
                if i >= 8:
                    p0_moved(pe, products[i - 8])
                product(q).then_inc(s["p0_psum"], 1)

            phase0_over(pe)
            pe.wait_ge(s["pad_ready"], 1)
            pe.wait_ge(s["ld_small"], 64)

            tiles_due = counter(pe, "xnT_sbuf", 2 * TG + 1, 1)

            def transpose_x(j, p, t):
                wait(pe, "xn_ready", num(j, p, t) + 1)
                for k in range(KC):
                    last = transpose(pt_ps[:, HKP + k * P:HKP + (k + 1) * P], xn[:, t, k * P:(k + 1) * P])
                return last

            transpose_x(0, 0, 0).then_inc(s["xt_psum"], 1)

            def batch(j, p):
                return j

            def step(j, p, t):
                n = num(j, p, t)
                b = batch(j, p)
                if live(j, p):
                    wait(pe, "shifted", n)
                    tiles_due(n + 1)
                    for c in range(0, HK, BANK):
                        w = min(BANK, HK - c)
                        mm(scores_ps[:, c:c + w], ones3[:, :], bias3[:, bass.ds(b, 1), c:c + w], start=True, stop=False)
                        for k in range(KC):
                            last = mm(scores_ps[:, c:c + w], xnT[:, t % 2, k, :], A[:, k, bass.ds(b, 1), c:c + w],
                                      start=False, stop=k == KC - 1)
                    last.then_inc(s["scores_psum"], 1)
                jh, ph = ago(j, p, 1)
                j2, p2 = ago(j, p, 2)

                def transpose_rows(half):
                    for tt in range(2):
                        for k in range(KC):
                            last = transpose(m_ps[:, (k * 2 + tt) * P:(k * 2 + tt + 1) * P],
                                             rows[:, ph, half * 2 + tt, k * P:(k + 1) * P])
                    last.then_inc(s["xn2T_psum"], 1)

                if t == 3 and live(jh, ph):
                    wait(pe, "pos_sbuf", num(jh, ph))
                    wait(pe, "rows_ready", num(jh, ph) * TG + 2)
                    transpose_rows(0)
                if t == 1 and live(j2, p2):
                    wait(pe, "earlier_ready", num(j2, p2))
                    wait(pe, "logits_sbuf", num(j2, p2) + 1)
                    wait(pe, "mask_ready", num(j2, p2) + 1)
                    for tt in range(TG):
                        counts = m_ps[:, tt * E:(tt + 1) * E]
                        mm(counts, before[:, :], mask[:, tt, :], start=True, stop=False)
                        for earlier in range(tt):
                            mm(counts, onesb[:, :], mask[:, earlier, :], start=False, stop=False)
                        last = mm(counts, onesb[:, :], before_sum[:, p2, :], start=False, stop=True)
                    last.then_inc(s["prefix_psum"], 1)
                jm, pm, tm = tile_ago(j, p, t, 1)
                jn, pn, tn = tile_ago(j, p, t, -1)
                if live(jm, pm):
                    m = num(jm, pm, tm)
                    wait(pe, "pT_sbuf", m * 3)
                    wait(pe, "probs_ready", m + 1)
                    for c in range(CK):
                        last = transpose(pt_ps[:, c * P:(c + 1) * P], sm[:, tm % 2, c * P:(c + 1) * P])
                        if c in (3, 7):
                            last.then_inc(s["pt_psum"], 1)
                if live(jn, pn) and live(j, p):
                    last = transpose_x(jn, pn, tn)
                if live(jm, pm) or live(j, p):
                    last.then_inc(s["xt_psum"], 1)
                if t == 3 and live(jh, ph):
                    wait(pe, "xn2T_sbuf", num(jh, ph) * 2 + 1)
                    wait(pe, "rows_ready", num(jh, ph) * TG + 4)
                    transpose_rows(1)
                jo, po, to = tile_ago(j, p, t, 2)
                if live(jo, po):
                    m = num(jo, po, to)
                    wait(pe, "res_ready", m)
                    for c in range(CK):
                        if c % 4 == 0:
                            wait(pe, "pT_sbuf", m * 3 + (c // 4 + 1))
                        last = mm(o_ps[:, 0:D], pT[:, to % 2, c, :], VO[:, bass.ds(batch(jo, po), 1), c, :],
                                  start=c == 0, stop=c == CK - 1)
                    last.then_inc(s["out_psum"], 1)
                if t == 3 and live(jh, ph):
                    wait(pe, "xn2T_sbuf", num(jh, ph) * 2 + 2)
                    for tt in range(TG):
                        for k in range(KC):
                            last = mm(m_ps[:, tt * E:(tt + 1) * E], xn2T[:, k, tt * P:(tt + 1) * P], wg[:, k, :],
                                      start=k == 0, stop=k == KC - 1)
                    last.then_inc(s["logits_psum"], 1)

            phase1(pe, step)

            pe.wait_ge(s["earlier_ready"], NG)
            pe.wait_ge(s["pos_sbuf"], NG)
            mm(m_ps[:, 0:E], onesb[:, :], before_sum[:, NG % 2, :], start=True, stop=True).then_inc(s["count_psum"], 1)

            phase1_over(pe)

            def s_up(g, c):
                if g:
                    pe.wait_ge(s["s_gated"], 2 * (g - 1) + c + 1)
                for i in range(2):
                    for k in range(KC):
                        last = mm(bank(2 * i + c), ws13[:, k, i * HS + c * P:i * HS + (c + 1) * P], xg[:, g % 2, k, :],
                                  start=k == 0, stop=k == KC - 1)
                last.then_inc(s["s_psum"], 1)

            def s_down(g):
                pe.wait_ge(s["s_gated"], 2 * g + 2)
                for t in range(TG):
                    if g and t % 2 == 0:
                        pe.wait_ge(s["z_sbuf"], 2 * (g - 1) + t // 2 + 1)
                    for c in range(KC):
                        last = mm(bank(4 + t // 2)[:, t % 2 * D:(t % 2 + 1) * D], sh[:, c, t * P:(t + 1) * P],
                                  ws2[:, c, :], start=c == 0, stop=c == KC - 1)
                    if t % 2:
                        last.then_inc(s["z_psum"], 1)

            for g in range(NG):
                pe.wait_ge(ld_xg[g % 2], 16 * (g // 2 + 1))
                s_up(g, 0)
                if g:
                    s_down(g - 1)
                s_up(g, 1)
                if g == 0:
                    pe.wait_ge(s["tab_step"], TAB_OPS)
                    for i in range(2):
                        n = min(P, BLOCKS - i * P)
                        last = transpose(o_ps[0:3, i * P:i * P + n], tabf[0:n, i, :])
                    last.then_inc(s["tab_psum"], 1)
            s_down(NG - 1)

            pe.wait_ge(s["early_w"], 16 * 5)
            pe.wait_ge(s["late_w"], 16 * 5 * 3)
            pe.wait_ge(s["tab_ready"], 1)
            pe.wait_ge(s["z_sbuf"], 2 * NG)

            def block_T(i, q, _):
                b = i * NX + q
                wait(pe, "xbT_sbuf", b - 1)
                wait(pe, ld_x[q], (i + 1) * 16)
                for k in range(KC):
                    last = transpose(bank(q % 2)[:, k * P:(k + 1) * P], xblk[:, q, k * P:(k + 1) * P])
                last.then_inc(s["xbT_psum"], 1)

            def block_up(i, q, e):
                b = i * NX + q
                wait(pe, "eh_ready", b - 1)
                wait(pe, "xbT_sbuf", b + 1)
                for k in range(KC):
                    last = mm(bank(2 + q % 2)[:, 0:2 * H], xbT[:, q % 2, k, :],
                              ew[:, bass.ds(e, 1), k * 2 * H:(k + 1) * 2 * H], start=k == 0, stop=k == KC - 1)
                last.then_inc(s["eh_psum"], 1)

            def block_hT(i, q, _):
                b = i * NX + q
                wait(pe, "ehT_sbuf", b - 1)
                wait(pe, "eh_ready", b + 1)
                transpose(bank(4 + q % 2)[:, 0:P], eh[:, q % 2, :]).then_inc(s["ehT_psum"], 1)

            def block_down(i, q, e):
                b = i * NX + q
                wait(pe, "eo_ready", b - 1)
                wait(pe, "ehT_sbuf", b + 1)
                mm(bank(6 + q % 2)[:, 0:D], ehT[:, q % 2, :], ew[:, bass.ds(e, 1), 2 * D:3 * D], start=True, stop=True
                   ).then_inc(s["eo_psum"], 1)

            turns(pe, {0: block_T, 1: block_up, 2: block_hT, LAG: block_down}, (1, 0, LAG, 2),
                  table(pe, "expert", 1, LAG + NX, E - 1))


TAB_OPS = 17


_INS = ["x", "ctx_1024"] + ["L0_xattn_" + n for n in ("Wq", "bq", "Wk", "bk", "Wv", "bv", "Wo", "bo", "gamma", "beta")] \
    + ["L0_ffn_" + n for n in ("Wg", "W1", "W2", "W3", "Ws1", "Ws2", "Ws3")]


def kernel(**inputs):
    import numpy as _np
    import concourse.bacc as _bacc
    from concourse import mybir as _mybir
    from concourse.bass_utils import run_bass_kernel_spmd as _run

    nc = _bacc.Bacc("TRN2", target_bir_lowering=False, num_devices=1)
    arrays, args = {}, []
    for name in _INS:
        a = _np.ascontiguousarray(inputs[name])
        arrays[f"in_{name}"] = a
        args.append(nc.dram_tensor(f"in_{name}", a.shape, _mybir.dt.from_np(a.dtype), kind="ExternalInput").ap())
    shape = inputs["x"].shape
    args.append(nc.dram_tensor("out_y", shape, _mybir.dt.float32, kind="ExternalOutput").ap())
    attention_moe_kernel(nc, *args)
    r = _run(nc, [arrays], core_ids=[0])
    return r.results[0]["out_y"]
```

```python
from contextlib import ExitStack

import concourse.bass as bass
from concourse import mybir

F32 = mybir.dt.float32
BF16 = mybir.dt.bfloat16
I32 = mybir.dt.int32
U32 = mybir.dt.uint32
ALU = mybir.AluOpType
ACT = mybir.ActivationFunctionType
AX = mybir.AxisListType.X

P = 128
BANK = 512
RSQRT_SEED = 0x5F3759DF
NEWTON = 3
RSQRT_OPS = 3 + 3 * NEWTON


def attention_moe_kernel(nc, x, ctx, Wq, bq, Wk, bk, Wv, bv, Wo, bo, gamma, beta,
                         Wg, W1, W2, W3, Ws1, Ws2, Ws3, out):
    B, S, D = x.shape
    SK = ctx.shape[1]
    HD = Wq.shape[1]
    DH = 64
    NH = HD // DH
    E, _, H = W1.shape
    HS = Ws1.shape[1]
    TOPK = 4
    EPS_LN, EPS_ATT = 1e-5, 1e-3
    T = B * S
    KC = D // P
    HP = HD // P
    HK = NH * SK
    CK = (HK + P - 1) // P
    HKP = CK * P
    BK = B * SK
    HB = BANK // SK
    SB = -(-NH // HB)
    SKE = SK + SK % 2
    TG = 4
    GT = TG * P
    NT = T // P
    NG = NT // TG
    CAP = 4 * T * TOPK // E
    REG = CAP + P
    DUMMY = E * REG
    TRASH = DUMMY + P
    ROW = D + E
    NX = 8
    BLOCKS = -(-((T * TOPK + E * (P - 1)) // P) // NX) * NX
    LAG = 3
    TURNS = BLOCKS // NX
    YPAIRS = TOPK * T
    YROWS = YPAIRS + 2 * E * P
    EW = 3 * D
    EARLY = 5
    assert YPAIRS == NT * GT and NG == 2 * B and KC == 2 and HS == 2 * P and H == P and SB == 3 and BLOCKS <= 2 * P and TG * D == E * E and P % E == 0 and E & (E - 1) == 0

    xt = x.rearrange("b s d -> (b s) d")
    ot = out.rearrange("b s d -> (b s) d")
    lists = nc.dram_tensor("expert_lists", [TRASH + P, ROW], F32, kind="Internal").ap()
    xn2T_d = nc.dram_tensor("xn2T_d", [NG, P, KC * GT], F32, kind="Internal").ap()
    x2_d = nc.dram_tensor("x2_d", [T, D], F32, kind="Internal").ap()
    base_d = nc.dram_tensor("base_d", [T, D], F32, kind="Internal").ap()
    y_d = nc.dram_tensor("y_d", [YROWS, D], F32, kind="Internal").ap()

    with ExitStack() as stack:
        def sb(name, shape, dt=F32, scope=stack):
            return scope.enter_context(nc.sbuf_tensor(name, shape, dt))

        def sem(name):
            return stack.enter_context(nc.semaphore(name))

        big = sb("big", [P, E * EW])
        ew = big[:, :].rearrange("p (e n) -> p e n", e=E)
        a_at = EARLY * EW
        vo_at = a_at + KC * B * HK
        A = big[:, a_at:vo_at].rearrange("p (k b n) -> p k b n", k=KC, b=B)
        VO = big[:, vo_at:vo_at + B * CK * D].rearrange("p (b c n) -> p b c n", b=B, c=CK)
        wq_sb = big[:, 0:KC * HD].rearrange("p (k n) -> p k n", k=KC)
        xs = big[:, KC * HD:KC * HD + TG * D].rearrange("p (t d) -> p t d", t=TG)
        assert KC * HD + TG * D <= a_at and vo_at + B * CK * D <= E * EW
        ident = sb("ident", [P, P])
        identb = sb("identb", [P, P], BF16)
        before = sb("before", [P, P], BF16)
        onesb = sb("onesb", [P, P], BF16)
        iota_e = sb("iota_e", [P, E])
        region = sb("region", [P, E])
        region0 = sb("region0", [P, E])
        trash_p = sb("trash_p", [P, 1])
        block_i = sb("block_i", [P, 2])
        block_m = sb("block_m", [P, 2], I32)
        block_e = sb("block_e", [P, 2], I32)
        bias3 = sb("bias3", [3, B, HK], BF16)
        ones3 = sb("ones3", [3, P], BF16)
        ln1 = sb("ln1", [P, NT, 2])
        wg = sb("wg", [P, KC, E])
        ws13 = sb("ws13", [P, KC, 2 * HS])
        ws2 = sb("ws2", [P, KC, D])
        gamma_b = sb("gamma_b", [P, D])
        beta_b = sb("beta_b", [P, D])
        zero = sb("zero", [P, D])
        filler = sb("filler", [P, ROW])
        dummy_rows = sb("dummy_rows", [P, ROW])
        wtop = sb("wtop", [P, NT, TOPK])
        pair = sb("pair", [P, TG, TOPK])
        before_sum = sb("before_sum", [P, 2, E], BF16)

        p0 = ExitStack()
        ctx_sb = sb("ctx_sb", [SK, B, D], scope=p0)
        ctxT = sb("ctxT", [P, KC, BK], scope=p0)
        wk_sb = sb("wk_sb", [P, KC, HD], scope=p0)
        wv_sb = sb("wv_sb", [P, KC, HD], scope=p0)
        wo_sb = sb("wo_sb", [P, HP, D], scope=p0)
        NB = 3 * HP + KC
        bias_rows = sb("bias_rows", [NB, P], scope=p0)
        biasT = sb("biasT", [P, NB], scope=p0)
        bo_h = sb("bo_h", [P, KC], scope=p0)
        bq2 = sb("bq2", [P, HP, 2], scope=p0)
        wqT = sb("wqT", [P, HP, D], scope=p0)
        kT = sb("kT", [P, HP, BK], scope=p0)
        vT = sb("vT", [P, HP, BK], scope=p0)
        voT = sb("voT", [P, B, HKP], scope=p0)
        sbias = sb("sbias", [SK, B, 3, NH], BF16, scope=p0)
        sres = sb("sres", [SK, 2, B, NH], scope=p0)
        sbiasT = sb("sbiasT", [3 * NH, B, SK], BF16, scope=p0)
        st1 = sb("st1", [P, NT, 6], scope=p0)
        mv1 = sb("mv1", [P, NT, 2], scope=p0)
        nw1 = sb("nw1", [P, 4, NT], scope=p0)
        p0.close()

        xin = sb("xin", [P, TG, D])
        xn = sb("xn", [P, TG, D])
        sm = sb("sm", [P, 2, HKP])
        pT = sb("pT", [P, 2, CK, P])
        x2g = (xin[:, :, :], xn[:, :, :])
        xg = pT[:, :, 0:KC * TG, :].rearrange("p i (k c) n -> p i k (c n)", k=KC)
        sg = sm[:, 0, 0:KC * GT].rearrange("p (k n) -> p k n", k=KC)
        sh = sm[:, 1, 0:KC * GT].rearrange("p (k n) -> p k n", k=KC)
        count = sb("count", [P, E])
        fill_at = sb("fill_at", [P, E], I32)
        nblk_i = sb("nblk_i", [P, 2, E], I32)
        nblk = sb("nblk", [P, E])
        upto = sb("upto", [P, E, E])
        blocks_upto = sb("blocks_upto", [P, E])
        past = sb("past", [P, 2, E])
        pastn = sb("pastn", [P, 2, E])
        tabw = sb("tabw", [P, 8, 2])
        tabf = sb("tabf", [P, 2, 3])
        tab = sb("tab", [3, LAG + BLOCKS + NX], I32)
        p1 = ExitStack()
        xnT = sb("xnT", [P, 2, KC, P], scope=p1)
        nmax = sb("nmax", [P, 2, NH], scope=p1)
        ssum = sb("ssum", [P, 2, NH], scope=p1)
        sinv = sb("sinv", [P, 2, NH], scope=p1)
        res = sb("res", [P, TG, D], scope=p1)
        scaled = sb("scaled", [P, TG, D], scope=p1)
        xres = sb("xres", [P, 2, TG, D], scope=p1)
        x2 = sb("x2", [P, 2, TG, D], scope=p1)
        rows = sb("rows", [P, 2, TG, ROW], scope=p1)
        xn2T = sb("xn2T", [P, KC, GT], scope=p1)
        ln1g = sb("ln1g", [P, 2, TG, 2], scope=p1)
        st2 = sb("st2", [P, TG, 6], scope=p1)
        mv2 = sb("mv2", [P, TG, 2], scope=p1)
        nw2 = sb("nw2", [P, 4, TG], scope=p1)
        st3 = sb("st3", [P, TG, 6], scope=p1)
        mv3 = sb("mv3", [P, TG, 2], scope=p1)
        nw3 = sb("nw3", [P, 4, TG], scope=p1)
        nmr3 = sb("nmr3", [P, TG], scope=p1)
        logits = sb("logits", [P, TG, E], scope=p1)
        lmax = sb("lmax", [P, TG], scope=p1)
        lsum = sb("lsum", [P, TG], scope=p1)
        linv = sb("linv", [P, TG], scope=p1)
        lexp = sb("lexp", [P, TG, E], scope=p1)
        prob = sb("prob", [P, TG, E], scope=p1)
        top = sb("top", [P, TG, 8], scope=p1)
        topi = sb("topi", [P, TG, 8], U32, scope=p1)
        topf = sb("topf", [P, TG, TOPK], scope=p1)
        onehot = sb("onehot", [P, TG, TOPK, E], scope=p1)
        mask = sb("mask", [P, TG, E], BF16, scope=p1)
        gsum = sb("gsum", [P, E], scope=p1)
        pos = sb("pos", [P, TG, E], scope=p1)
        valid = sb("valid", [P, TG, E], scope=p1)
        base_e = sb("base_e", [P, TG, E], scope=p1)
        slot_e = sb("slot_e", [P, TG, E], scope=p1)
        pairs_e = sb("pairs_e", [P, TG, TOPK, E], scope=p1)
        picked = sb("picked", [P, TG, TOPK, E], scope=p1)
        slotf = sb("slotf", [P, TG, TOPK], scope=p1)
        slot = sb("slot", [P, 2, TG, TOPK], U32, scope=p1)
        nupto = scaled[:, :, :].rearrange("p t d -> p (t d)").rearrange("p (e f) -> p e f", e=E)
        p1.close()

        xblk = sb("xblk", [P, NX, ROW])
        xbT = sb("xbT", [P, 2, KC, P])
        eg = sb("eg", [P, 2, H])
        eh = sb("eh", [P, 2, H])
        ehT = sb("ehT", [P, 2, P])
        eo = sb("eo", [P, NX, D])
        yrow = sb("yrow", [P, NX], U32)
        ysum = big[:, 0:2 * (TOPK + 1) * GT * D // P].rearrange("p (i k t d) -> p i k t d", i=2, k=TOPK + 1, t=TG)
        final = sb("final", [P, 2, TG, D])

        psum = stack.enter_context(nc.psum_tensor("psum", [P, 8 * BANK], F32))

        def bank(i, n=1):
            return psum[:, i * BANK:(i + n) * BANK]

        scores_ps, pt_ps, o_ps, m_ps = bank(0, 3), bank(3, 3), bank(6), bank(7)

        def head_scores(h0, h1):
            at = h0 // HB * BANK + h0 % HB * SK
            return scores_ps[:, at:at + (h1 - h0) * SK]

        s = {n: sem(n) for n in """consts_raw consts upto_raw upto_ready
            ld_ctx ld_bias ld_wq ld_wk ld_wv ld_wo ld_bc ld_small ld_xs early_w late_w zeroed dummy_filled
            p0_psum p0_act p0_dve bo_h_ready bq2_ready voT_padded split_step sbias_moved
            ln1_stats ln1_aggr ln1_step ln1_ready ln1g_ready pad_ready
            xn_ready xt_psum xnT_sbuf scores_psum nmax_ready exped inverted probs_ready
            pt_psum pT_sbuf out_psum res_ready res_stats mv2_ready scaled_ready ln2_step xb_ready x2_ready
            x2_stats mv3_ready ln3_step nmr3_ready rows_ready xn2T_psum xn2T_sbuf xn2T_stored
            logits_psum logits_sbuf lmax_ready lshifted lexped lsum_ready linv_ready prob_ready top_ready topi_ready
            topf_ready onehot_ready mask_ready gsum_ready earlier_ready prefix_psum pos_sbuf valid_ready base_ready
            slot_e_ready picked_ready slotf_ready slot_ready pairs_e_ready rows_of_y_ready pair_ready weights_ready
            count_psum tab_step fill_ready tab_psum tab_ready
            s_psum s_silu s_gated z_psum z_added
            xbT_psum xbT_sbuf eh_psum eg_ready eh_ready ehT_psum ehT_sbuf yrow_ready eo_psum eo_ready
            ysum_step""".split()}
        ld_xin = [sem(f"ld_xin{t}") for t in range(TG)]
        ld_xres = [sem(f"ld_xres{p}") for p in range(2)]
        filled = [sem(f"filled{n}") for n in range(2)]
        lists_ready = [sem(f"lists_ready{p}") for p in range(2)]
        x2_stored = [sem(f"x2_stored{p}") for p in range(2)]
        ld_xg = [sem(f"ld_xg{p}") for p in range(2)]
        ld_x = [sem(f"ld_xblk{i}") for i in range(NX)]
        scattered = [sem(f"scattered{i}") for i in range(NX)]
        ld_x2g = [sem(f"ld_x2g{p}") for p in range(2)]
        base_stored = [sem(f"base_stored{p}") for p in range(2)]
        ld_y = [sem(f"ld_y{p}") for p in range(2)]
        stored = [sem(f"stored{p}") for p in range(2)]

        def wait(eng, name, n):
            if not isinstance(n, int) or n > 0:
                eng.wait_ge(s[name] if isinstance(name, str) else name, n)

        def counter(eng, name, first, by):
            due = eng.alloc_register(f"due_{name}")
            eng.reg_mov(due, first)

            def wait_due(n):
                if isinstance(n, int):
                    wait(eng, name, n)
                else:
                    eng.wait_ge(s[name], due)
                    eng.reg_add(due, due, by)
            return wait_due

        def ago(j, p, d):
            return j + (p - d) // 2, (p - d) % 2

        def live(j, p):
            return not isinstance(j, int) or 0 <= 2 * j + p < NG

        def tile_ago(j, p, t, d):
            return (*ago(j, p, -((t - d) // TG)), (t - d) % TG)

        def num(j, p, t=None):
            return j * 2 + p if t is None else j * (2 * TG) + (p * TG + t)

        def wrap(n, size):
            return n if isinstance(n, int) else n % size

        def phase1(eng, step):
            for g in range(2):
                for t in range(TG):
                    step(0, g, t)
            with eng.Fori(1, NG // 2) as j:
                for p in range(2):
                    for t in range(TG):
                        step(j, p, t)

        def drain(step, first, last):
            for n in range(first, last + 1):
                step(NG // 2, n // TG, n % TG)

        def shared_rest(eng, step):
            with eng.Fori(2, NG // 2) as i:
                for p in range(2):
                    step(i, p)

        def turns(eng, stages, order, load_turn=None):
            def turn(i, qs, skip):
                of_turn = load_turn(i) if load_turn else None
                for q in qs:
                    for lag in order:
                        if not skip(q, lag):
                            stages[lag](i + (q - lag) // NX, (q - lag) % NX, of_turn and of_turn(q, lag))

            turn(0, range(NX), lambda q, lag: q < lag)
            with eng.Fori(1, TURNS) as i:
                turn(i, range(NX), lambda q, lag: False)
            turn(TURNS, range(LAG), lambda q, lag: q >= lag)

        def table(eng, name, row, n, max_val):
            regs = [eng.alloc_register(f"{name}{k}") for k in range(n)]

            def load_turn(i):
                eng.reg_load(regs, tab[row:row + 1, bass.ds(i * NX, n)])
                values = [eng.snap(r, min_val=0, max_val=max_val) for r in regs]
                return lambda q, lag: values[q - lag + LAG] if q - lag + LAG < n else None
            return load_turn

        def fill_lists(eng, half):
            eng.wait_ge(s["fill_ready"], 1)
            per = E // 4
            regs = [eng.alloc_register(f"fill{k}") for k in range(per)]
            for e in range(half * E // 2, (half + 1) * E // 2, per):
                eng.reg_load(regs, fill_at[0:1, e:e + per])
                for r in regs:
                    at = eng.snap(r, min_val=0, max_val=DUMMY - P)
                    eng.dma_start(lists[bass.ds(at, P), :], filler[:, :]).then_inc(filled[half], 16)

        products = [("bias",)]
        products += [("ctx", b) for b in range(B)]
        products += [("k", j) for j in range(HP)]
        products += [("wq", j) for j in range(HP)]
        products += [("sbias",)]
        products += [("a", d, h) for h in range(NH) for d in range(KC)]
        products += [("sbiasT",)]
        products += [("v", j) for j in range(HP)]
        for d in range(KC):
            products += [("vo", d, h) for h in range(NH)]
            products += [("voT", d, b, c) for b in range(B) for c in range(0, CK, 4)]
        number = {q: i for i, q in enumerate(products)}
        mover = {q: "dve" if i % 2 or q[0][:5] == "sbias" else "act" for i, q in enumerate(products)}
        moved_by = {e: [q for q in products if mover[q] == e] for e in ("act", "dve")}

        def p0_moved(eng, *qs):
            for e in ("act", "dve"):
                last = max((moved_by[e].index(q) for q in qs if mover[q] == e), default=None)
                if last is not None:
                    eng.wait_ge(s["p0_" + e], last + 1)

        def p0_bank(q):
            return bank(number[q] % 8)

        def phase0_over(eng):
            eng.wait_ge(s["ln1_ready"], 1)
            eng.wait_ge(s["sbias_moved"], 16 * 3 * B)
            eng.wait_ge(s["p0_act"], len(moved_by["act"]))
            eng.wait_ge(s["p0_dve"], len(moved_by["dve"]))

        def phase1_over(eng):
            for p in range(2):
                eng.wait_ge(lists_ready[p], 16 * TG * TOPK * NG // 2)
                eng.wait_ge(x2_stored[p], 16 * NG // 2)
            eng.wait_ge(s["xn2T_stored"], 16 * NG)
            eng.wait_ge(s["weights_ready"], NG)
            eng.wait_ge(s["xnT_sbuf"], NT + 1)

        block = stack.enter_context(nc.Block())

        @block.sync
        def _(sp):
            sp.dma_start(ctx_sb[:, :, :], ctx.rearrange("b k d -> k b d")).then_inc(s["ld_ctx"], 16)
            for i, v in enumerate((bq, bk, bv, bo)):
                n = v.shape[0] // P
                sp.dma_start(bias_rows[i * HP:i * HP + n, :], v.rearrange("(c p) -> c p", p=P)
                             ).then_inc(s["ld_bias"], 16)
            for w_sb, w, name in ((wk_sb[:, :, :], Wk, "ld_wk"), (wq_sb, Wq, "ld_wq"), (wv_sb[:, :, :], Wv, "ld_wv")):
                sp.dma_start(w_sb, w.rearrange("(k p) n -> p k n", p=P)).then_inc(s[name], 16)
            sp.dma_start(wo_sb[:, :, :], Wo.rearrange("(c p) n -> p c n", p=P)).then_inc(s["ld_wo"], 16)
            for t_sb, v in ((gamma_b, gamma), (beta_b, beta)):
                sp.dma_start(t_sb[:, :], v.partition_broadcast(P)).then_inc(s["ld_bc"], 16)
            for g in range(NG):
                if g:
                    sp.wait_ge(s["ln1_stats"], g * TG)
                sp.dma_start(xs, xt[g * GT:(g + 1) * GT, :].rearrange("(t p) d -> p t d", p=P)
                             ).then_inc(s["ld_xs"], 16)
            sp.dma_start(wg[:, :, :], Wg.rearrange("(k p) n -> p k n", p=P)).then_inc(s["ld_small"], 16)
            for i, w in enumerate((Ws1, Ws3)):
                sp.dma_start(ws13[:, :, i * HS:(i + 1) * HS], w.rearrange("(k p) n -> p k n", p=P)
                             ).then_inc(s["ld_small"], 16)
            sp.dma_start(ws2[:, :, :], Ws2.rearrange("(k p) n -> p k n", p=P)).then_inc(s["ld_small"], 16)

            sp.wait_ge(s["p0_dve"], moved_by["dve"].index(("sbiasT",)) + 1)
            for i in range(3):
                for b in range(B):
                    sp.dma_start(bias3[i:i + 1, b, :].rearrange("o (h k) -> o h k", h=NH),
                                 sbiasT[i * NH:(i + 1) * NH, b, :]).then_inc(s["sbias_moved"], 16)

            phase0_over(sp)

            def load_x(j, p, t):
                sp.dma_start(xin[:, t, :], xt[bass.ds(wrap(num(j, p, t), NT) * P, P), :]).then_inc(ld_xin[t], 16)

            for t in range(TG):
                load_x(0, 0, t)

            def load_experts(e0, e1, name):
                for k in range(KC):
                    for i, w in enumerate((W1, W3)):
                        at = (2 * k + i) * H
                        sp.dma_start(ew[:, e0:e1, at:at + H], w[e0:e1, k * P:(k + 1) * P, :].rearrange("e p n -> p e n")
                                     ).then_inc(s[name], 16)
                sp.dma_start(ew[:, e0:e1, 2 * D:3 * D], W2[e0:e1].rearrange("e p n -> p e n")).then_inc(s[name], 16)

            load_experts(0, EARLY, "early_w")
            sp.wait_ge(s["consts"], 1)
            sp.dma_start(lists[DUMMY:DUMMY + P, :], dummy_rows[:, :]).then_inc(s["dummy_filled"], 16)

            def step(j, p, t):
                jn, pn = ago(j, p, -1)
                if live(j, p) and live(jn, pn):
                    wait(sp, "xn_ready", num(j, p, t) + 1)
                    load_x(jn, pn, t)
                if live(j, p):
                    sp.dma_start(y_d[bass.ds(num(j, p, t) * GT, GT), :].rearrange("(p r) d -> p r d", p=P),
                                 zero[:, :].unsqueeze(1).to_broadcast([P, TG, D])).then_inc(s["zeroed"], 16)
                if t == 2 and live(j, p):
                    wait(sp, "x2_ready", num(*ago(j, p, 1)) * TG)
                    sp.dma_start(xres[:, p, :, :], xt[bass.ds(num(j, p) * GT, GT), :]
                                 .rearrange("(t p) d -> p t d", p=P)).then_inc(ld_xres[p], 16)
                if t == 3 and live(*ago(j, p, 1)):
                    jh, ph = ago(j, p, 1)
                    wait(sp, "x2_ready", (num(jh, ph) + 1) * TG)
                    sp.dma_start(x2_d[bass.ds(num(jh, ph) * GT, GT), :].rearrange("(t p) d -> p t d", p=P),
                                 x2[:, ph, :, :]).then_inc(x2_stored[ph], 16)
                if t == 1 and live(*ago(j, p, 2)):
                    jh, ph = ago(j, p, 2)
                    wait(sp, "xn2T_sbuf", (num(jh, ph) + 1) * 2)
                    sp.dma_start(xn2T_d[bass.ds(num(jh, ph), 1), :, :].rearrange("o p n -> (o p) n"),
                                 xn2T[:, :, :].rearrange("p k n -> p (k n)")).then_inc(s["xn2T_stored"], 16)

            phase1(sp, step)

            def store_base(i, p):
                wait(sp, "z_added", (num(i, p) + 1) * 2)
                sp.dma_start(base_d[bass.ds(num(i, p) * GT, GT), :].rearrange("(t p) d -> p t d", p=P), x2g[p]
                             ).then_inc(base_stored[p], 16)

            def load_shared(i, p):
                g = num(i, p)
                wait(sp, "s_psum", (g - 1) * 2)
                sp.dma_start(xg[:, p, :, :], xn2T_d[bass.ds(g, 1), :, :].rearrange("o p (k n) -> (o p) k n", k=KC)
                             ).then_inc(ld_xg[p], 16)
                if not isinstance(i, int) or i:
                    store_base(i - 1, p)
                wait(sp, base_stored[p], i * 16)
                sp.dma_start(x2g[p], x2_d[bass.ds(g * GT, GT), :].rearrange("(t p) d -> p t d", p=P)
                             ).then_inc(ld_x2g[p], 16)

            drain(step, 0, 1)
            sp.wait_ge(s["out_psum"], NT)
            for t in range(TG):
                sp.wait_ge(ld_xin[t], 16 * (NG + 1))
            sp.wait_ge(s["xn_ready"], NT + 2)
            sp.wait_ge(s["xt_psum"], NT + 1)
            sp.wait_ge(s["res_ready"], NT)
            for p in range(2):
                sp.wait_ge(x2_stored[p], 16 * (NG // 2 - p))
            sp.wait_ge(s["xn2T_stored"], 16 * (NG - 1))
            for p in range(2):
                load_shared(0, p)
            sp.wait_ge(s["scores_psum"], NT * SB)
            late = E - EARLY
            for e in range(EARLY, E, late // 3):
                load_experts(e, e + late // 3, "late_w")
            drain(step, 2, 2 * TG - 1)
            load_shared(1, 0)
            fill_lists(sp, 0)
            load_shared(1, 1)
            sp.wait_ge(x2_stored[1], 16 * NG // 2)
            sp.wait_ge(s["xn2T_stored"], 16 * NG)
            shared_rest(sp, load_shared)

            for n in range(2):
                sp.wait_ge(filled[n], 16 * E // 2)
            sp.wait_ge(s["dummy_filled"], 16)
            sp.wait_ge(s["tab_ready"], 1)
            rows_of = table(sp, "first_row", 0, LAG + NX, DUMMY)

            def load_turn(i, of_turn):
                for q in range(NX):
                    wait(sp, "xbT_psum", (i - 1) * NX + (q + 1))
                    wait(sp, "yrow_ready", (i - 1) * NX + (q + 1))
                    sp.dma_start(xblk[:, q, :], lists[bass.ds(of_turn(q, 0), P), :]).then_inc(ld_x[q], 16)

            phase1_over(sp)
            load_turn(0, rows_of(0))
            for p in range(2):
                store_base(NG // 2 - 1, p)
            with sp.Fori(1, TURNS) as i:
                load_turn(i, rows_of(i))

            sp.wait_ge(s["eo_psum"], BLOCKS)
            for q in range(NX):
                sp.wait_ge(scattered[q], 16 * TURNS)
            for p in range(2):
                sp.wait_ge(base_stored[p], 16 * NG // 2)

            def load_y(i, p):
                for k in range(TOPK + 1):
                    src = y_d[bass.ds(num(i, p) * GT + k * T, GT), :] if k < TOPK else base_d[bass.ds(num(i, p) * GT, GT), :]
                    sp.dma_start(ysum[:, p, k, :, :], src.rearrange("(t p) d -> p t d", p=P)).then_inc(ld_y[p], 16)

            def store_final(i, p):
                wait(sp, "ysum_step", (num(i, p) + 1) * (TOPK * TG))
                sp.dma_start(ot[bass.ds(num(i, p) * GT, GT), :].rearrange("(t p) d -> p t d", p=P), final[:, p, :, :]
                             ).then_inc(stored[p], 16)

            for p in range(2):
                load_y(0, p)
            with sp.Fori(1, NG // 2) as i:
                for p in range(2):
                    store_final(i - 1, p)
                    load_y(i, p)
            for p in range(2):
                store_final(NG // 2 - 1, p)
            for p in range(2):
                sp.wait_ge(stored[p], 16 * NG // 2)

        @block.gpsimd
        def _(pool):
            kw = dict(allow_small_or_imprecise_dtypes=True)
            raw = [pool.memset(ident[:, :], 0.0),
                   pool.memset(before[:, :], 1.0),
                   pool.memset(onesb[:, :], 1.0),
                   pool.memset(ones3[:, :], 1.0),
                   pool.memset(zero[:, :], 0.0),
                   pool.memset(filler[:, :], 0.0),
                   pool.memset(before_sum[:, :, :], 0.0),
                   pool.iota(iota_e[:, :], [[1, E]], base=0, channel_multiplier=0, **kw),
                   pool.iota(region[:, :], [[REG, E]], base=-TRASH, channel_multiplier=-1, **kw),
                   pool.iota(region0[:, :], [[REG, E]], base=0, channel_multiplier=0, **kw),
                   pool.iota(trash_p[:, :], [[0, 1]], base=TRASH, channel_multiplier=1, **kw),
                   pool.iota(block_m[:, :], [[P, 2]], base=0, channel_multiplier=1),
                   pool.iota(block_i[:, :], [[P, 2]], base=0, channel_multiplier=1, **kw),
                   pool.iota(pair[:, :, :], [[P, TG], [T, TOPK]], base=0, channel_multiplier=1, **kw),
                   pool.memset(dummy_rows[:, :], 0.0)]
            for ins in raw:
                ins.then_inc(s["consts_raw"], 1)
            pool.wait_ge(s["consts_raw"], len(raw))
            for rows_sb, at in ((filler, YPAIRS), (dummy_rows, YPAIRS + E * P)):
                pool.iota(rows_sb[:, D:ROW].bitcast(I32), [[P, E]], base=at, channel_multiplier=1
                          ).then_inc(s["consts_raw"], 1)
            pool.affine_select(out=ident[:, :], in_=ident[:, :], compare_op=ALU.not_equal, fill=1.0, base=0,
                               pattern=[[-1, P]], channel_multiplier=1).then_inc(s["consts_raw"], 1)
            pool.affine_select(out=before[:, :], in_=before[:, :], compare_op=ALU.is_gt, fill=0.0, base=0,
                               pattern=[[1, P]], channel_multiplier=-1).then_inc(s["consts_raw"], 1)
            pool.wait_ge(s["consts_raw"], len(raw) + 4)
            pool.tensor_copy(identb[:, :], ident[:, :]).then_inc(s["consts"], 1)

            phase0_over(pool)
            pool.memset(upto[:, :, :], 1.0).then_inc(s["upto_raw"], 1)
            pool.wait_ge(s["upto_raw"], 1)
            pool.affine_select(out=upto[:, :, :], in_=upto[:, :, :], compare_op=ALU.is_ge, fill=0.0, base=0,
                               pattern=[[1, E], [-1, E]], channel_multiplier=0).then_inc(s["upto_ready"], 1)
            pool.wait_ge(s["ld_bc"], 32)
            slots_due = counter(pool, "slot_ready", 1, 1)

            def step(j, p, t):
                if live(j, p):
                    wait(pool, "inverted", num(j, p, t) + 1)
                    e3 = sm[:, t % 2, 0:HK].rearrange("p (h k) -> p h k", h=NH)
                    pool.tensor_tensor(e3, e3, sinv[:, t % 2, :].unsqueeze(2).to_broadcast([P, NH, SK]), ALU.mult
                                       ).then_inc(s["probs_ready"], 1)
                if t == 0 and live(*ago(j, p, 1)):
                    jh, ph = ago(j, p, 1)
                    wait(pool, ld_xres[ph], (jh + 1) * 16)
                    pool.tensor_tensor(xres[:, ph, :, :], xres[:, ph, :, :],
                                       beta_b[:, :].unsqueeze(1).to_broadcast([P, TG, D]), ALU.add
                                       ).then_inc(s["xb_ready"], 1)
                if t >= 2 and live(*ago(j, p, 2)):
                    jh, ph = ago(j, p, 2)
                    if t == 2:
                        wait(pool, "rows_ready", (num(jh, ph) + 1) * TG)
                        wait(pool, "rows_of_y_ready", num(jh, ph) + 1)
                        slots_due(num(jh, ph) + 1)
                    for tt in ((0, 1) if t == 2 else (2, 3)):
                        for k in range(TOPK):
                            pool.indirect_dma_start(
                                out=lists, out_offset=bass.IndirectOffsetOnAxis(ap=slot[:, ph, tt, k:k + 1], axis=0),
                                in_=rows[:, ph, tt, :], in_offset=None).then_inc(lists_ready[ph], 16)

            phase1(pool, step)
            drain(step, 0, 2 * TG - 1)

            pool.wait_ge(s["zeroed"], 16 * NT)
            outputs_due = counter(pool, "eo_ready", NX + 1, 1)

            def scatter_block(i, q):
                wait(pool, "yrow_ready", i * NX + (q + 1))
                outputs_due(i * NX + (q + 1))
                pool.indirect_dma_start(
                    out=y_d, out_offset=bass.IndirectOffsetOnAxis(ap=yrow[:, q:q + 1], axis=0),
                    in_=eo[:, q, :], in_offset=None).then_inc(scattered[q], 16)

            for q in range(NX):
                scatter_block(0, q)
            with pool.Fori(1, TURNS) as i:
                for q in range(NX):
                    scatter_block(i, q)

        def p0_copy(eng, dst, src, bias=None):
            if eng == "act":
                if bias is None:
                    return nc.scalar.activation(dst, src, ACT.Copy)
                return nc.scalar.activation(dst, src, ACT.Identity, bias=bias)
            if bias is None:
                return nc.vector.tensor_copy(dst, src)
            return nc.vector.tensor_scalar(dst, src, bias, None, ALU.add)

        def p0_move(e, q):
            src, kind = p0_bank(q), q[0]
            if kind == "bias":
                return p0_copy(e, biasT[:, :], src[:, 0:NB])
            if kind == "ctx":
                return p0_copy(e, ctxT[:, :, q[1] * SK:(q[1] + 1) * SK],
                               src[:, 0:KC * SK].rearrange("p (k n) -> p k n", k=KC))
            if kind == "wq":
                return p0_copy(e, wqT[:, q[1], :], src[:, 0:D])
            if kind == "k":
                return p0_copy(e, kT[:, q[1], :], src[:, 0:BK], biasT[:, HP + q[1]:HP + q[1] + 1])
            if kind == "v":
                return p0_copy(e, vT[:, q[1], :], src[:, 0:BK], biasT[:, 2 * HP + q[1]:2 * HP + q[1] + 1])
            if kind == "a":
                return p0_copy(e, A[:, q[1], :, q[2] * SK:(q[2] + 1) * SK],
                               src[:, 0:BK].rearrange("p (b n) -> p b n", b=B))
            if kind == "vo":
                return p0_copy(e, voT[:, :, q[2] * SK:(q[2] + 1) * SK],
                               src[:, 0:BK].rearrange("p (b n) -> p b n", b=B), bo_h[:, q[1]:q[1] + 1])
            if kind == "voT":
                _, d, b, c = q
                n = min(4, CK - c)
                return p0_copy(e, VO[:, b, c:c + n, d * P:(d + 1) * P],
                               src[:, 0:n * P].rearrange("p (c n) -> p c n", c=n))
            if kind == "sbiasT":
                return p0_copy(e, sbiasT[:, :, :], src.bitcast(BF16)[0:3 * NH, 0:B * SKE]
                               .rearrange("p (b k) -> p b k", b=B)[:, :, 0:SK])
            raise AssertionError(q)

        @block.scalar
        def _(act):
            for q in moved_by["act"]:
                act.wait_ge(s["p0_psum"], number[q] + 1)
                if q[0] in ("k", "v"):
                    p0_moved(act, ("bias",))
                if q[0] == "vo":
                    act.wait_ge(s["bo_h_ready"], 1)
                p0_move("act", q).then_inc(s["p0_act"], 1)

            def norm_x(j, p, t):
                wait(act, "ln1g_ready", num(j, p) + 1)
                wait(act, "res_ready", num(j, p, t) + (1 - TG))
                wait(act, ld_xin[t], (num(j, p) + 1) * 16)
                nc.scalar.activation(xn[:, t, :], xin[:, t, :], ACT.Identity, scale=ln1g[:, p, t, 0:1],
                                     bias=ln1g[:, p, t, 1:2]).then_inc(s["xn_ready"], 1)

            def move_xnT(j, p, t):
                wait(act, "scores_psum", (num(j, p, t) - 1) * SB)
                wait(act, "xt_psum", num(j, p, t) + 1)
                nc.scalar.activation(xnT[:, t % 2, :, :].rearrange("p k n -> p (k n)"), pt_ps[:, HKP:HKP + D], ACT.Copy
                                     ).then_inc(s["xnT_sbuf"], 1)

            def move_xn2T(jh, ph, half):
                g = num(jh, ph)
                wait(act, "xn2T_stored", g * 16)
                wait(act, "xn2T_psum", g * 2 + (half + 1))
                nc.scalar.activation(xn2T[:, :, half * 2 * P:(half + 1) * 2 * P],
                                     m_ps.rearrange("p (k n) -> p k n", k=KC), ACT.Copy).then_inc(s["xn2T_sbuf"], 1)

            phase0_over(act)
            norm_x(0, 0, 0)
            norm_x(0, 0, 1)
            move_xnT(0, 0, 0)

            def step(j, p, t):
                jh, ph = ago(j, p, 1)
                j2, p2 = ago(j, p, 2)
                if t == 1 and live(j2, p2):
                    wait(act, "slot_e_ready", num(j2, p2))
                    wait(act, "prefix_psum", num(j2, p2) + 1)
                    nc.scalar.activation(pos[:, :, :].rearrange("p t e -> p (t e)"), m_ps[:, 0:TG * E], ACT.Copy
                                         ).then_inc(s["pos_sbuf"], 1)
                if t == 3 and live(jh, ph):
                    move_xn2T(jh, ph, 0)
                jn, pn, tn = tile_ago(j, p, t, -1)
                if live(j, p) and live(jn, pn):
                    move_xnT(jn, pn, tn)
                if t == 0 and live(j2, p2):
                    wait(act, "lshifted", num(j2, p2) + 1)
                    nc.scalar.activation(lexp[:, :, :], lexp[:, :, :], ACT.Exp).then_inc(s["lexped"], 1)
                if live(j, p):
                    n = num(j, p, t)
                    wait(act, "inverted", n - 1)
                    wait(act, "pt_psum", (n - 1) * 3)
                    for h in range(NH):
                        if h % HB == 0:
                            wait(act, "nmax_ready", n * 2 + (1 if h < 2 * HB else 2))
                        last = nc.scalar.activation(sm[:, t % 2, h * SK:(h + 1) * SK], head_scores(h, h + 1), ACT.Exp,
                                                    bias=nmax[:, t % 2, h:h + 1], accum_out=ssum[:, t % 2, h:h + 1])
                        if h % HB == HB - 1 or h == NH - 1:
                            last.then_inc(s["exped"], 1)
                if t == 3 and live(jh, ph):
                    move_xn2T(jh, ph, 1)
                jm, pm, tm = tile_ago(j, p, t, 1)
                if live(jm, pm):
                    m = num(jm, pm, tm)
                    for c in range(0, CK, 4):
                        wait(act, "out_psum", m - 1)
                        wait(act, "pt_psum", m * 3 + (c // 4 + 1))
                        k = min(4, CK - c)
                        nc.scalar.activation(pT[:, tm % 2, c:c + k, :].rearrange("p c n -> p (c n)"),
                                             pt_ps[:, c * P:(c + k) * P], ACT.Copy).then_inc(s["pT_sbuf"], 1)
                jx, px, tx = tile_ago(j, p, t, -2)
                if live(jx, px):
                    norm_x(jx, px, tx)
                if t == 3 and live(jh, ph):
                    wait(act, "lshifted", num(jh, ph))
                    wait(act, "logits_psum", num(jh, ph) + 1)
                    nc.scalar.activation(logits[:, :, :].rearrange("p t e -> p (t e)"), m_ps[:, 0:TG * E], ACT.Copy
                                         ).then_inc(s["logits_sbuf"], 1)
                if t == 2 and live(jh, ph):
                    for tt in range(TG):
                        wait(act, lists_ready[ph], jh * (16 * TG * TOPK))
                        wait(act, "nmr3_ready", num(jh, ph) + 1)
                        nc.scalar.activation(rows[:, ph, tt, 0:D], x2[:, ph, tt, :], ACT.Identity,
                                             scale=nw3[:, 2, tt:tt + 1], bias=nmr3[:, tt:tt + 1]
                                             ).then_inc(s["rows_ready"], 1)

            phase1(act, step)
            drain(step, 0, 1)

            def shared_silu(i, p, c):
                g = num(i, p)
                wait(act, "s_gated", (g - 1) * 2 + (c + 1))
                wait(act, "s_psum", g * 2 + (c + 1))
                nc.scalar.activation(sg[:, c, :], bank(c), ACT.Silu).then_inc(s["s_silu"], 1)

            def shared_step(i, p):
                for c in range(KC):
                    shared_silu(i, p, c)

            act.wait_ge(s["pt_psum"], NT * 3)
            shared_step(0, 0)
            drain(step, 2, TG)
            shared_step(0, 1)
            drain(step, TG + 1, 2 * TG - 1)
            shared_step(1, 0)
            fill_lists(act, 1)
            shared_step(1, 1)
            shared_rest(act, shared_step)

            phase1_over(act)

            def silu(i, q, _):
                b = i * NX + q
                wait(act, "eh_ready", b - 1)
                wait(act, "eh_psum", b + 1)
                nc.scalar.activation(eg[:, q % 2, :], bank(2 + q % 2)[:, 0:H], ACT.Silu).then_inc(s["eg_ready"], 1)

            def move_eo(i, q, _):
                wait(act, scattered[q], i * 16)
                wait(act, "eo_psum", i * NX + (q + 1))
                nc.scalar.activation(eo[:, q, :], bank(6 + q % 2)[:, 0:D], ACT.Copy).then_inc(s["eo_ready"], 1)

            turns(act, {1: silu, LAG: move_eo}, (1, LAG))

        def rsqrt(dve, name, base, var, eps, w):
            def after(i):
                dve.wait_ge(s[name], base + i)

            nc.vector.tensor_scalar(w[:, 0, :], var, eps, None, ALU.add).then_inc(s[name], 1)
            after(1)
            nc.vector.tensor_scalar(w[:, 1, :].bitcast(I32), w[:, 0, :].bitcast(I32), 1, None, ALU.logical_shift_right
                                    ).then_inc(s[name], 1)
            after(2)
            nc.vector.tensor_scalar(w[:, 2, :].bitcast(I32), w[:, 1, :].bitcast(I32), -1.0, float(RSQRT_SEED),
                                    ALU.mult, ALU.add).then_inc(s[name], 1)
            for k in range(NEWTON):
                after(3 + 3 * k)
                nc.vector.tensor_tensor(w[:, 3, :], w[:, 2, :], w[:, 2, :], ALU.mult).then_inc(s[name], 1)
                after(4 + 3 * k)
                nc.vector.scalar_tensor_tensor(w[:, 1, :], w[:, 3, :], -0.5, w[:, 0, :], ALU.mult, ALU.mult
                                               ).then_inc(s[name], 1)
                after(5 + 3 * k)
                nc.vector.scalar_tensor_tensor(w[:, 2, :], w[:, 1, :], 1.5, w[:, 2, :], ALU.add, ALU.mult
                                               ).then_inc(s[name], 1)

        @block.vector
        def _(dve):
            def stats1(g):
                dve.wait_ge(s["ld_xs"], 16 * (g + 1))
                for t in range(g * TG, (g + 1) * TG):
                    nc.vector.bn_stats(st1[:, t, :], xs[:, t % TG, :]).then_inc(s["ln1_stats"], 1)
                for t in range(g * TG, (g + 1) * TG):
                    dve.wait_ge(s["ln1_stats"], t + 1)
                    nc.vector.bn_aggr(mv1[:, t, :], st1[:, t, :]).then_inc(s["ln1_aggr"], 1)

            def split_bias(q):
                src = p0_bank(q)[0:SK, 0:B * NH].rearrange("k (b h) -> k b h", b=B)
                steps = [lambda: nc.vector.tensor_copy(sbias[:, :, 0, :], src),
                         lambda: nc.vector.tensor_tensor(sres[:, 0], src, sbias[:, :, 0, :], ALU.subtract),
                         lambda: nc.vector.tensor_copy(sbias[:, :, 1, :], sres[:, 0]),
                         lambda: nc.vector.tensor_tensor(sres[:, 1], sres[:, 0], sbias[:, :, 1, :], ALU.subtract),
                         lambda: nc.vector.tensor_copy(sbias[:, :, 2, :], sres[:, 1])]
                for i, step in enumerate(steps):
                    if i:
                        dve.wait_ge(s["split_step"], i)
                    ins = step()
                    ins.then_inc(s["split_step"] if i < len(steps) - 1 else s["p0_dve"], 1)

            nc.vector.memset(bq2[:, :, :], 0.0).then_inc(s["bq2_ready"], 1)
            nc.vector.memset(voT[:, :, HK:HKP], 0.0).then_inc(s["voT_padded"], 1)
            stats_at = {("a", 1, h): g for g, h in enumerate(range(1, NH, 2))}
            for q in products:
                if q[0] == "ctx" and q[1] == B - 1:
                    p0_moved(dve, ("bias",))
                    dve.wait_ge(s["bq2_ready"], 1)
                    for i in range(2):
                        half = slice(i * DH, (i + 1) * DH)
                        nc.vector.tensor_copy(bq2[half, :, i], biasT[half, 0:HP]).then_inc(s["bq2_ready"], 1)
                    nc.vector.tensor_scalar(bo_h[:, :], biasT[:, 3 * HP:NB], 1.0 / NH, None, ALU.mult
                                            ).then_inc(s["bo_h_ready"], 1)
                if mover[q] == "dve":
                    dve.wait_ge(s["p0_psum"], number[q] + 1)
                    if q[0] in ("k", "v"):
                        p0_moved(dve, ("bias",))
                    if q[0] == "vo":
                        dve.wait_ge(s["bo_h_ready"], 1)
                    if q[0] == "sbias":
                        split_bias(q)
                    else:
                        p0_move("dve", q).then_inc(s["p0_dve"], 1)
                if q in stats_at:
                    stats1(stats_at[q])
            dve.wait_ge(s["ln1_aggr"], NT)
            rsqrt(dve, "ln1_step", 0, mv1[:, :, 1], EPS_LN, nw1)
            dve.wait_ge(s["ln1_step"], RSQRT_OPS)
            nc.vector.tensor_copy(ln1[:, :, 0], nw1[:, 2, :]).then_inc(s["ln1_step"], 1)
            dve.wait_ge(s["ln1_step"], RSQRT_OPS + 1)
            nc.vector.scalar_tensor_tensor(ln1[:, :, 1], mv1[:, :, 0], -1.0, nw1[:, 2, :], ALU.mult, ALU.mult
                                           ).then_inc(s["ln1_ready"], 1)

            phase0_over(dve)
            nc.vector.memset(sm[:, :, HK:HKP], 0.0).then_inc(s["pad_ready"], 1)

            res_stats_due = counter(dve, "res_stats", 2 * TG, TG)
            x2_stats_due = counter(dve, "x2_stats", 2 * TG, TG)
            probs_due = counter(dve, "prob_ready", 1, 1)
            tops_due = counter(dve, "top_ready", TG, TG)

            def group_ln1(j, p):
                wait(dve, "xn_ready", (num(j, p) - 1) * TG)
                nc.vector.tensor_scalar(ln1g[:, p, :, :], ln1[:, bass.ds(wrap(num(j, p), NG) * TG, TG), :], 1.0, None, ALU.mult
                                        ).then_inc(s["ln1g_ready"], 1)

            group_ln1(0, 0)

            def second_norm(jh, ph):
                g = num(jh, ph)
                res_stats_due((g + 1) * TG)
                for t in range(TG):
                    nc.vector.bn_aggr(mv2[:, t, :], st2[:, t, :]).then_inc(s["mv2_ready"], 1)
                for t in range(TG):
                    wait(dve, "mv2_ready", g * TG + (t + 1))
                    wait(dve, "x2_ready", (g - 1) * TG + (t + 1))
                    nc.vector.scalar_tensor_tensor(scaled[:, t, :], res[:, t, :], mv2[:, t, 0:1], gamma_b[:, :],
                                                   ALU.subtract, ALU.mult).then_inc(s["scaled_ready"], 1)
                rsqrt(dve, "ln2_step", g * RSQRT_OPS, mv2[:, :, 1], EPS_ATT, nw2)

            def third_norm(jh, ph):
                g = num(jh, ph)
                wait(dve, "xb_ready", g + 1)
                wait(dve, "ln2_step", (g + 1) * RSQRT_OPS)
                for t in range(TG):
                    wait(dve, "scaled_ready", g * TG + (t + 1))
                    wait(dve, x2_stored[ph], jh * 16)
                    wait(dve, "rows_ready", (g - 1) * TG)
                    nc.vector.scalar_tensor_tensor(x2[:, ph, t, :], scaled[:, t, :], nw2[:, 2, t:t + 1],
                                                   xres[:, ph, t, :], ALU.mult, ALU.add).then_inc(s["x2_ready"], 1)
                for t in range(TG):
                    wait(dve, "x2_ready", g * TG + (t + 1))
                    nc.vector.bn_stats(st3[:, t, :], x2[:, ph, t, :]).then_inc(s["x2_stats"], 1)
                x2_stats_due((g + 1) * TG)
                for t in range(TG):
                    nc.vector.bn_aggr(mv3[:, t, :], st3[:, t, :]).then_inc(s["mv3_ready"], 1)
                wait(dve, "rows_ready", g * TG)
                wait(dve, "mv3_ready", (g + 1) * TG)
                rsqrt(dve, "ln3_step", g * RSQRT_OPS, mv3[:, :, 1], EPS_LN, nw3)
                wait(dve, "ln3_step", (g + 1) * RSQRT_OPS)
                nc.vector.scalar_tensor_tensor(nmr3[:, :], mv3[:, :, 0], -1.0, nw3[:, 2, :], ALU.mult, ALU.mult
                                               ).then_inc(s["nmr3_ready"], 1)

            def over_e(a):
                return a.unsqueeze(2).to_broadcast([P, TG, E])

            def shift_logits(jh, ph):
                g = num(jh, ph)

                wait(dve, "logits_sbuf", g + 1)
                nc.vector.tensor_reduce(lmax[:, :], logits[:, :, :], AX, ALU.max).then_inc(s["lmax_ready"], 1)
                wait(dve, "lmax_ready", g + 1)
                nc.vector.tensor_tensor(lexp[:, :, :], logits[:, :, :], over_e(lmax[:, :]), ALU.subtract
                                        ).then_inc(s["lshifted"], 1)

            def choose(jh, ph):
                g = num(jh, ph)
                wait(dve, "lexped", g + 1)
                nc.vector.tensor_reduce(lsum[:, :], lexp[:, :, :], AX, ALU.add).then_inc(s["lsum_ready"], 1)
                wait(dve, "lsum_ready", g + 1)
                nc.vector.reciprocal(linv[:, :], lsum[:, :]).then_inc(s["linv_ready"], 1)
                wait(dve, "linv_ready", g + 1)
                nc.vector.tensor_tensor(prob[:, :, :], lexp[:, :, :], over_e(linv[:, :]), ALU.mult
                                        ).then_inc(s["prob_ready"], 1)
                probs_due(g + 1)
                for t in range(TG):
                    nc.vector.max(top[:, t, :], prob[:, t, :]).then_inc(s["top_ready"], 1)
                tops_due((g + 1) * TG)
                for t in range(TG):
                    nc.vector.max_index(topi[:, t, :], top[:, t, :], prob[:, t, :]).then_inc(s["topi_ready"], 1)
                wait(dve, "topi_ready", (g + 1) * TG)
                nc.vector.tensor_copy(topf[:, :, :], topi[:, :, 0:TOPK]).then_inc(s["topf_ready"], 1)
                wait(dve, "topf_ready", g + 1)
                nc.vector.tensor_tensor(onehot[:, :, :, :].rearrange("p t k e -> p (t k) e"),
                                        iota_e[:, :].unsqueeze(1).to_broadcast([P, TG * TOPK, E]),
                                        topf[:, :, :].rearrange("p t k -> p (t k)").unsqueeze(2)
                                        .to_broadcast([P, TG * TOPK, E]), ALU.is_equal).then_inc(s["onehot_ready"], 1)
                wait(dve, "onehot_ready", g + 1)
                with nc.allow_low_precision(reason="sums of at most one 1"):
                    nc.vector.tensor_reduce(mask[:, :, :], onehot[:, :, :, :].rearrange("p t k e -> p t e k"), AX,
                                            ALU.add).then_inc(s["mask_ready"], 1)
                wait(dve, "mask_ready", g + 1)
                nc.vector.tensor_reduce(gsum[:, :], mask[:, :, :].rearrange("p t e -> p e t"), AX, ALU.add
                                        ).then_inc(s["gsum_ready"], 1)
                wait(dve, "pair_ready", g)
                nc.vector.tensor_tensor(pairs_e[:, :, :, :].rearrange("p t k e -> p (t k) e"),
                                        onehot[:, :, :, :].rearrange("p t k e -> p (t k) e"),
                                        pair[:, :, :].rearrange("p t k -> p (t k)").unsqueeze(2)
                                        .to_broadcast([P, TG * TOPK, E]), ALU.mult).then_inc(s["pairs_e_ready"], 1)
                wait(dve, "prefix_psum", g)
                wait(dve, "gsum_ready", g + 1)
                nc.vector.tensor_tensor(before_sum[:, 1 - ph, :], before_sum[:, ph, :], gsum[:, :], ALU.add
                                        ).then_inc(s["earlier_ready"], 1)
                wait(dve, "pairs_e_ready", g + 1)
                nc.vector.tensor_scalar(pair[:, :, :], pair[:, :, :], float(GT), None, ALU.add).then_inc(s["pair_ready"], 1)
                wait(dve, lists_ready[ph], jh * (16 * TG * TOPK))
                with nc.allow_low_precision(reason="whole numbers, sums of one of them and zeros"):
                    nc.vector.tensor_reduce(rows[:, ph, :, D:ROW].bitcast(I32),
                                            pairs_e[:, :, :, :].rearrange("p t k e -> p t e k"), AX, ALU.add
                                            ).then_inc(s["rows_of_y_ready"], 1)
                nc.vector.tensor_scalar(wtop[:, bass.ds(g * TG, TG), :], top[:, :, 0:TOPK], 1.0, None, ALU.mult
                                        ).then_inc(s["weights_ready"], 1)

            def place(jh, ph):
                g = num(jh, ph)
                wait(dve, "pos_sbuf", g + 1)
                nc.vector.tensor_scalar(valid[:, :, :], pos[:, :, :], float(CAP), None, ALU.is_lt
                                        ).then_inc(s["valid_ready"], 1)
                nc.vector.tensor_tensor(base_e[:, :, :], pos[:, :, :],
                                        region[:, :].unsqueeze(1).to_broadcast([P, TG, E]), ALU.add
                                        ).then_inc(s["base_ready"], 1)
                wait(dve, "base_ready", g + 1)
                nc.vector.tensor_tensor(slot_e[:, :, :], base_e[:, :, :], valid[:, :, :], ALU.mult
                                        ).then_inc(s["slot_e_ready"], 1)
                wait(dve, "slot_e_ready", g + 1)
                nc.vector.tensor_tensor(picked[:, :, :, :], onehot[:, :, :, :],
                                        slot_e[:, :, :].unsqueeze(2).to_broadcast([P, TG, TOPK, E]), ALU.mult
                                        ).then_inc(s["picked_ready"], 1)
                wait(dve, "picked_ready", g + 1)
                nc.vector.tensor_reduce(slotf[:, :, :], picked[:, :, :, :], AX, ALU.add).then_inc(s["slotf_ready"], 1)
                wait(dve, "slotf_ready", g + 1)
                nc.vector.tensor_scalar(slot[:, ph, :, :], slotf[:, :, :], trash_p[:, 0:1], None, ALU.add
                                        ).then_inc(s["slot_ready"], 1)

            def step(j, p, t):
                n = num(j, p, t)
                heads = "p (h k) -> p h k"
                if t == 0 and live(*ago(j, p, 2)):
                    shift_logits(*ago(j, p, 2))
                if live(j, p):
                    wait(dve, "exped", (n - 1) * SB)
                    for i, (h0, h1) in enumerate(((0, 2 * HB), (2 * HB, NH))):
                        wait(dve, "scores_psum", n * SB + 2 + i)
                        sc = (scores_ps[:, 0:2 * BANK].rearrange("p (b n) -> p b n", b=2)[:, :, 0:HB * SK]
                              .rearrange("p b (h k) -> p b h k", h=HB) if i == 0 else
                              head_scores(h0, h1).rearrange(heads, h=h1 - h0))
                        mx = nmax[:, t % 2, h0:h1]
                        nc.vector.tensor_reduce(mx.rearrange("p (b h) -> p b h", b=2) if i == 0 else mx, sc, AX, ALU.max,
                                                negate=True).then_inc(s["nmax_ready"], 1)
                if t == 1 and live(*ago(j, p, -1)) and live(j, p):
                    group_ln1(*ago(j, p, -1))
                if t == 0 and live(*ago(j, p, 2)):
                    choose(*ago(j, p, 2))
                if t == 1 and live(*ago(j, p, 2)):
                    place(*ago(j, p, 2))
                if t == 2 and live(*ago(j, p, 1)):
                    third_norm(*ago(j, p, 1))
                jm, pm, tm = tile_ago(j, p, t, 2)
                if live(jm, pm):
                    m = num(jm, pm, tm)
                    wait(dve, "scaled_ready", m + 1 - TG)
                    wait(dve, "out_psum", m + 1)
                    nc.vector.tensor_tensor(res[:, tm, :], o_ps[:, 0:D], xn[:, tm, :], ALU.add
                                            ).then_inc(s["res_ready"], 1)
                    wait(dve, "res_ready", m + 1)
                    nc.vector.bn_stats(st2[:, tm, :], res[:, tm, :]).then_inc(s["res_stats"], 1)
                if t == 1 and live(*ago(j, p, 1)):
                    second_norm(*ago(j, p, 1))
                if live(j, p):
                    wait(dve, "probs_ready", n - 1)
                    wait(dve, "exped", (n + 1) * SB)
                    nc.vector.reciprocal(sinv[:, t % 2, :], ssum[:, t % 2, :]).then_inc(s["inverted"], 1)

            phase1(dve, step)
            drain(step, 0, 2)

            def shared_gate(i, p):
                g = num(i, p)
                for c in range(KC):
                    wait(dve, "z_psum", g * 2)
                    wait(dve, "s_silu", g * 2 + (c + 1))
                    nc.vector.tensor_tensor(sh[:, c, :], sg[:, c, :], bank(2 + c), ALU.mult).then_inc(s["s_gated"], 1)

            def add_shared(i, p):
                wait(dve, ld_x2g[p], i * 16 + 16)
                for half in range(2):
                    wait(dve, "z_psum", num(i, p) * 2 + (half + 1))
                    x2_half = x2g[p][:, 2 * half:2 * half + 2, :].rearrange("p t d -> p (t d)")
                    nc.vector.tensor_tensor(x2_half, x2_half, bank(4 + half), ALU.add).then_inc(s["z_added"], 1)

            def shared_step(i, p):
                if live(*ago(i, p, 1)):
                    add_shared(*ago(i, p, 1))
                if live(i, p):
                    shared_gate(i, p)

            dve.wait_ge(s["pt_psum"], NT * 3)
            shared_step(0, 0)
            drain(step, 3, TG)
            shared_step(0, 1)
            drain(step, TG + 1, 2 * TG - 1)

            tab_ops = [0]

            def tab_op(ins):
                ins.then_inc(s["tab_step"], 1)
                tab_ops[0] += 1
                dve.wait_ge(s["tab_step"], tab_ops[0])

            tab_op(nc.vector.memset(tab[:, :], 0))
            dve.wait_ge(s["count_psum"], 1)
            tab_op(nc.vector.tensor_scalar(count[:, :], m_ps[:, 0:E], float(CAP), None, ALU.min))
            nc.vector.tensor_tensor(fill_at[:, :], count[:, :], region0[:, :], ALU.add).then_inc(s["fill_ready"], 1)
            tab_op(nc.vector.tensor_scalar(nblk_i[:, 0, :], count[:, :], float(P - 1), None, ALU.add))
            tab_op(nc.vector.tensor_scalar(nblk_i[:, 1, :], nblk_i[:, 0, :], P.bit_length() - 1, None,
                                           ALU.logical_shift_right))
            tab_op(nc.vector.tensor_copy(nblk[:, :], nblk_i[:, 1, :]))
            dve.wait_ge(s["upto_ready"], 1)
            tab_op(nc.vector.tensor_tensor(nupto[:, :, :], upto[:, :, :],
                                           nblk[:, :].unsqueeze(1).to_broadcast([P, E, E]), ALU.mult))
            tab_op(nc.vector.tensor_reduce(blocks_upto[:, :], nupto[:, :, :], AX, ALU.add))
            tab_op(nc.vector.tensor_tensor(past[:, :, :], blocks_upto[:, :].unsqueeze(1).to_broadcast([P, 2, E]),
                                           block_i[:, :].unsqueeze(2).to_broadcast([P, 2, E]), ALU.is_le))
            tab_op(nc.vector.tensor_tensor(pastn[:, :, :], past[:, :, :],
                                           nblk[:, :].unsqueeze(1).to_broadcast([P, 2, E]), ALU.mult))
            expert, first, at, row, row1, past_end, turn_e, turned = (tabw[:, i, :] for i in range(8))
            tab_op(nc.vector.tensor_reduce(expert, past[:, :, :], AX, ALU.add))
            tab_op(nc.vector.tensor_reduce(first, pastn[:, :, :], AX, ALU.add))
            tab_op(nc.vector.tensor_tensor(at, block_i[:, :], first, ALU.subtract))
            tab_op(nc.vector.tensor_scalar(row, expert, float(REG), None, ALU.mult))
            tab_op(nc.vector.scalar_tensor_tensor(row1, at, float(P), row, ALU.mult, ALU.add))
            tab_op(nc.vector.tensor_scalar(tabf[:, :, 0], row1, float(DUMMY), None, ALU.min))
            tab_op(nc.vector.tensor_scalar(tabf[:, :, 1], expert, float(E - 1), None, ALU.min))
            tab_op(nc.vector.tensor_scalar(past_end, expert, float(E), None, ALU.is_ge))
            tab_op(nc.vector.tensor_scalar(block_e[:, :], block_m[:, :], E - 1, None, ALU.bitwise_and))
            tab_op(nc.vector.tensor_copy(turn_e, block_e[:, :]))
            tab_op(nc.vector.tensor_tensor(turned, past_end, turn_e, ALU.mult))
            tab_op(nc.vector.scalar_tensor_tensor(tabf[:, :, 2], tabf[:, :, 1], float(D), turned, ALU.add, ALU.subtract))

            shared_step(1, 0)
            dve.wait_ge(s["tab_psum"], 1)
            nc.vector.tensor_copy(tab[:, LAG:LAG + BLOCKS], o_ps[0:3, 0:BLOCKS]).then_inc(s["tab_ready"], 1)
            shared_step(1, 1)
            shared_rest(dve, shared_step)
            shared_step(NG // 2, 0)
            phase1_over(dve)

            def move_xbT(i, q, col):
                b = i * NX + q
                wait(dve, "eh_psum", b - 1)
                wait(dve, scattered[q], i * 16)
                wait(dve, "xbT_psum", b + 1)
                nc.vector.tensor_copy(xbT[:, q % 2, :, :].rearrange("p k n -> p (k n)"), bank(q % 2)[:, 0:D]
                                      ).then_inc(s["xbT_sbuf"], 1)
                nc.vector.tensor_copy(yrow[:, q:q + 1], xblk[:, q, bass.ds(col, 1)].bitcast(U32)
                                      ).then_inc(s["yrow_ready"], 1)

            def gate(i, q, _):
                b = i * NX + q
                wait(dve, "ehT_psum", b - 1)
                wait(dve, "eg_ready", b + 1)
                nc.vector.tensor_tensor(eh[:, q % 2, :], eg[:, q % 2, :], bank(2 + q % 2)[:, H:2 * H], ALU.mult
                                        ).then_inc(s["eh_ready"], 1)

            def move_ehT(i, q, _):
                b = i * NX + q
                wait(dve, "eo_psum", b - 1)
                wait(dve, "ehT_psum", b + 1)
                nc.vector.tensor_copy(ehT[:, q % 2, :], bank(4 + q % 2)[:, 0:P]).then_inc(s["ehT_sbuf"], 1)

            turns(dve, {0: move_xbT, 1: gate, 2: move_ehT}, (0, 2, 1), table(dve, "y_col", 2, LAG + NX, ROW - 1))

            def sum_group(i, p):
                g = num(i, p)
                wait(dve, ld_y[p], i * (16 * (TOPK + 1)) + 16 * (TOPK + 1))
                for k in range(TOPK):
                    for t in range(TG):
                        if k:
                            wait(dve, "ysum_step", g * (TOPK * TG) + ((k - 1) * TG + t + 1))
                        if k == TOPK - 1:
                            wait(dve, stored[p], i * 16)
                        out_sb = ysum[:, p, k, t, :] if k < TOPK - 1 else final[:, p, t, :]
                        nc.vector.scalar_tensor_tensor(out_sb, ysum[:, p, k, t, :], wtop[:, bass.ds(g * TG + t, 1), k],
                                                       ysum[:, p, k - 1 if k else TOPK, t, :], ALU.mult, ALU.add
                                                       ).then_inc(s["ysum_step"], 1)

            for p in range(2):
                sum_group(0, p)
            with dve.Fori(1, NG // 2) as i:
                for p in range(2):
                    sum_group(i, p)

        @block.tensor
        def _(pe):
            mm = nc.tensor.matmul

            def transpose(out, in_):
                n = in_.shape[0]
                return nc.tensor.transpose(out, in_, ident[0:n, 0:n])

            def product(q):
                ps, kind = p0_bank(q), q[0]
                if kind == "bias":
                    pe.wait_ge(s["ld_bias"], 64)
                    return transpose(ps[:, 0:NB], bias_rows[:, :])
                if kind == "ctx":
                    pe.wait_ge(s["ld_ctx"], 16)
                    for k in range(KC):
                        last = transpose(ps[:, k * SK:(k + 1) * SK], ctx_sb[:, q[1], k * P:(k + 1) * P])
                    return last
                if kind == "wq":
                    pe.wait_ge(s["ld_wq"], 16)
                    for k in range(KC):
                        last = transpose(ps[:, k * P:(k + 1) * P], wq_sb[:, k, q[1] * P:(q[1] + 1) * P])
                    return last
                if kind in "kv":
                    w_sb = wk_sb if kind == "k" else wv_sb
                    pe.wait_ge(s["ld_w" + kind], 16)
                    p0_moved(pe, *[("ctx", b) for b in range(B)])
                    for k in range(KC):
                        last = mm(ps[:, 0:BK], w_sb[:, k, q[1] * P:(q[1] + 1) * P], ctxT[:, k, :], start=k == 0,
                                  stop=k == KC - 1)
                    return last
                if kind == "sbias":
                    pe.wait_ge(s["bq2_ready"], 3)
                    p0_moved(pe, *[("k", j) for j in range(HP)])
                    for b in range(B):
                        for j in range(HP):
                            last = mm(ps[0:SK, b * NH + 2 * j:b * NH + 2 * j + 2], kT[:, j, b * SK:(b + 1) * SK],
                                      bq2[:, j, :], start=True, stop=True)
                    return last
                if kind == "sbiasT":
                    p0_moved(pe, ("sbias",))
                    for b in range(B):
                        last = nc.tensor.transpose(ps.bitcast(BF16)[0:3 * NH, b * SKE:b * SKE + SK],
                                                   sbias[:, b, :, :].rearrange("k i h -> k (i h)"), identb[0:SK, 0:SK])
                    return last
                if kind == "a":
                    _, d, h = q
                    half = slice(h % 2 * DH, (h % 2 + 1) * DH)
                    p0_moved(pe, ("wq", h // 2), ("k", h // 2))
                    return mm(ps[:, 0:BK], wqT[half, h // 2, d * P:(d + 1) * P], kT[half, h // 2, :], start=True,
                              stop=True)
                if kind == "vo":
                    _, d, h = q
                    half = slice(h % 2 * DH, (h % 2 + 1) * DH)
                    pe.wait_ge(s["ld_wo"], 16)
                    p0_moved(pe, ("v", h // 2))
                    return mm(ps[:, 0:BK], wo_sb[half, h // 2, d * P:(d + 1) * P], vT[half, h // 2, :], start=True,
                              stop=True)
                _, d, b, c = q
                pe.wait_ge(s["voT_padded"], 1)
                p0_moved(pe, *[("vo", d, h) for h in range(NH)])
                for i in range(min(4, CK - c)):
                    last = transpose(ps[:, i * P:(i + 1) * P], voT[:, b, (c + i) * P:(c + i + 1) * P])
                return last

            pe.wait_ge(s["consts"], 1)
            for i, q in enumerate(products):
                if i >= 8:
                    p0_moved(pe, products[i - 8])
                product(q).then_inc(s["p0_psum"], 1)

            phase0_over(pe)
            pe.wait_ge(s["pad_ready"], 1)
            pe.wait_ge(s["ld_small"], 64)

            def transpose_x(j, p, t):
                wait(pe, "xn_ready", num(j, p, t) + 1)
                for k in range(KC):
                    last = transpose(pt_ps[:, HKP + k * P:HKP + (k + 1) * P], xn[:, t, k * P:(k + 1) * P])
                return last

            transpose_x(0, 0, 0).then_inc(s["xt_psum"], 1)

            def batch(j, p):
                return j

            def step(j, p, t):
                n = num(j, p, t)
                b = batch(j, p)
                if live(j, p):
                    wait(pe, "xnT_sbuf", n + 1)
                    for c in range(SB):
                        h0, h1 = c * HB, min((c + 1) * HB, NH)
                        cols = slice(h0 * SK, h1 * SK)
                        wait(pe, "exped", (n - 1) * SB + (c + 1))
                        for k in range(KC):
                            mm(head_scores(h0, h1), xnT[:, t % 2, k, :], A[:, k, bass.ds(b, 1), cols], start=k == 0,
                               stop=False)
                        mm(head_scores(h0, h1), ones3[:, :], bias3[:, bass.ds(b, 1), cols], start=False, stop=True
                           ).then_inc(s["scores_psum"], 1)
                jh, ph = ago(j, p, 1)
                j2, p2 = ago(j, p, 2)

                def transpose_rows(jr, pr, half):
                    for tt in range(2):
                        for k in range(KC):
                            last = transpose(m_ps[:, (k * 2 + tt) * P:(k * 2 + tt + 1) * P],
                                             rows[:, pr, half * 2 + tt, k * P:(k + 1) * P])
                    last.then_inc(s["xn2T_psum"], 1)

                if t == 1 and live(j2, p2):
                    wait(pe, "earlier_ready", num(j2, p2))
                    wait(pe, "logits_sbuf", num(j2, p2) + 1)
                    wait(pe, "mask_ready", num(j2, p2) + 1)
                    for tt in range(TG):
                        counts = m_ps[:, tt * E:(tt + 1) * E]
                        mm(counts, before[:, :], mask[:, tt, :], start=True, stop=False)
                        for earlier in range(tt):
                            mm(counts, onesb[:, :], mask[:, earlier, :], start=False, stop=False)
                        last = mm(counts, onesb[:, :], before_sum[:, p2, :], start=False, stop=True)
                    last.then_inc(s["prefix_psum"], 1)
                if t == 3 and live(jh, ph):
                    wait(pe, "pos_sbuf", num(jh, ph))
                    wait(pe, "rows_ready", num(jh, ph) * TG + 2)
                    transpose_rows(jh, ph, 0)
                jm, pm, tm = tile_ago(j, p, t, 1)
                jn, pn, tn = tile_ago(j, p, t, -1)
                if live(jn, pn) and live(j, p):
                    wait(pe, "pT_sbuf", (n - 1) * 3)
                    transpose_x(jn, pn, tn).then_inc(s["xt_psum"], 1)
                jo, po, to = tile_ago(j, p, t, 2)
                if live(jo, po):
                    m = num(jo, po, to)
                    wait(pe, "res_ready", m)
                    for c in range(CK):
                        if c % 4 == 0:
                            wait(pe, "pT_sbuf", m * 3 + (c // 4 + 1))
                        last = mm(o_ps[:, 0:D], pT[:, to % 2, c, :], VO[:, bass.ds(batch(jo, po), 1), c, :],
                                  start=c == 0, stop=c == CK - 1)
                    last.then_inc(s["out_psum"], 1)
                if t == 3 and live(jh, ph):
                    wait(pe, "xn2T_sbuf", num(jh, ph) * 2 + 1)
                    wait(pe, "rows_ready", num(jh, ph) * TG + 4)
                    transpose_rows(jh, ph, 1)
                if live(jm, pm):
                    m = num(jm, pm, tm)
                    wait(pe, "pT_sbuf", m * 3)
                    wait(pe, "xnT_sbuf", min(m + 3, NT + 1) if isinstance(m, int) else m + 3)
                    wait(pe, "probs_ready", m + 1)
                    for c in range(CK):
                        last = transpose(pt_ps[:, c * P:(c + 1) * P], sm[:, tm % 2, c * P:(c + 1) * P])
                        if c % 4 == 3 or c == CK - 1:
                            last.then_inc(s["pt_psum"], 1)
                if t == 3 and live(jh, ph):
                    wait(pe, "xn2T_sbuf", num(jh, ph) * 2 + 2)
                    for tt in range(TG):
                        for k in range(KC):
                            last = mm(m_ps[:, tt * E:(tt + 1) * E], xn2T[:, k, tt * P:(tt + 1) * P], wg[:, k, :],
                                      start=k == 0, stop=k == KC - 1)
                    last.then_inc(s["logits_psum"], 1)

            phase1(pe, step)
            drain(step, 0, 1)

            pe.wait_ge(s["exped"], NT * SB)
            pe.wait_ge(s["pT_sbuf"], NT * 3)
            pe.wait_ge(s["xnT_sbuf"], NT + 1)

            def s_up(i, p, c):
                g = num(i, p)
                wait(pe, "s_gated", (g - 1) * 2 + (c + 1))
                for n in range(2):
                    for k in range(KC):
                        last = mm(bank(2 * n + c), ws13[:, k, n * HS + c * P:n * HS + (c + 1) * P], xg[:, p, k, :],
                                  start=k == 0, stop=k == KC - 1)
                last.then_inc(s["s_psum"], 1)

            def s_down(i, p):
                g = num(i, p)
                wait(pe, "s_gated", g * 2 + 2)
                for t in range(TG):
                    if t % 2 == 0:
                        wait(pe, "z_added", (g - 1) * 2 + (t // 2 + 1))
                    for c in range(KC):
                        last = mm(bank(4 + t // 2)[:, t % 2 * D:(t % 2 + 1) * D], sh[:, c, t * P:(t + 1) * P],
                                  ws2[:, c, :], start=c == 0, stop=c == KC - 1)
                    if t % 2:
                        last.then_inc(s["z_psum"], 1)

            def shared_step(i, p):
                if live(i, p):
                    wait(pe, ld_xg[p], i * 16 + 16)
                    s_up(i, p, 0)
                if live(*ago(i, p, 1)):
                    s_down(*ago(i, p, 1))
                if live(i, p):
                    s_up(i, p, 1)

            shared_step(0, 0)
            drain(step, 2, TG - 1)
            shared_step(0, 1)
            drain(step, TG, 2 * TG - 1)

            pe.wait_ge(s["earlier_ready"], NG)
            pe.wait_ge(s["pos_sbuf"], NG)
            mm(m_ps[:, 0:E], onesb[:, :], before_sum[:, NG % 2, :], start=True, stop=True).then_inc(s["count_psum"], 1)

            shared_step(1, 0)
            pe.wait_ge(s["res_ready"], NT)
            pe.wait_ge(s["tab_step"], TAB_OPS)
            for n in range(2):
                size = min(P, BLOCKS - n * P)
                last = transpose(o_ps[0:3, n * P:n * P + size], tabf[0:size, n, :])
            last.then_inc(s["tab_psum"], 1)
            shared_step(1, 1)
            shared_rest(pe, shared_step)
            shared_step(NG // 2, 0)

            pe.wait_ge(s["early_w"], 16 * 5)
            pe.wait_ge(s["late_w"], 16 * 5 * 3)
            pe.wait_ge(s["tab_ready"], 1)
            pe.wait_ge(s["z_added"], 2 * NG)

            def block_T(i, q, _):
                b = i * NX + q
                wait(pe, "xbT_sbuf", b - 1)
                wait(pe, ld_x[q], (i + 1) * 16)
                for k in range(KC):
                    last = transpose(bank(q % 2)[:, k * P:(k + 1) * P], xblk[:, q, k * P:(k + 1) * P])
                last.then_inc(s["xbT_psum"], 1)

            def block_up(i, q, e):
                b = i * NX + q
                wait(pe, "eh_ready", b - 1)
                wait(pe, "xbT_sbuf", b + 1)
                for k in range(KC):
                    last = mm(bank(2 + q % 2)[:, 0:2 * H], xbT[:, q % 2, k, :],
                              ew[:, bass.ds(e, 1), k * 2 * H:(k + 1) * 2 * H], start=k == 0, stop=k == KC - 1)
                last.then_inc(s["eh_psum"], 1)

            def block_hT(i, q, _):
                b = i * NX + q
                wait(pe, "ehT_sbuf", b - 1)
                wait(pe, "eh_ready", b + 1)
                transpose(bank(4 + q % 2)[:, 0:P], eh[:, q % 2, :]).then_inc(s["ehT_psum"], 1)

            def block_down(i, q, e):
                b = i * NX + q
                wait(pe, "eo_ready", b - 1)
                wait(pe, "ehT_sbuf", b + 1)
                mm(bank(6 + q % 2)[:, 0:D], ehT[:, q % 2, :], ew[:, bass.ds(e, 1), 2 * D:3 * D], start=True, stop=True
                   ).then_inc(s["eo_psum"], 1)

            turns(pe, {0: block_T, 1: block_up, 2: block_hT, LAG: block_down}, (0, 1, 2, LAG),
                  table(pe, "expert", 1, LAG + NX, E - 1))


TAB_OPS = 21


_INS = ["x", "ctx_1024"] + ["L0_xattn_" + n for n in ("Wq", "bq", "Wk", "bk", "Wv", "bv", "Wo", "bo", "gamma", "beta")] \
    + ["L0_ffn_" + n for n in ("Wg", "W1", "W2", "W3", "Ws1", "Ws2", "Ws3")]


def kernel(**inputs):
    import numpy as _np
    import concourse.bacc as _bacc
    from concourse import mybir as _mybir
    from concourse.bass_utils import run_bass_kernel_spmd as _run

    nc = _bacc.Bacc("TRN2", target_bir_lowering=False, num_devices=1)
    arrays, args = {}, []
    for name in _INS:
        a = _np.ascontiguousarray(inputs[name])
        arrays[f"in_{name}"] = a
        args.append(nc.dram_tensor(f"in_{name}", a.shape, _mybir.dt.from_np(a.dtype), kind="ExternalInput").ap())
    shape = inputs["x"].shape
    args.append(nc.dram_tensor("out_y", shape, _mybir.dt.float32, kind="ExternalOutput").ap())
    attention_moe_kernel(nc, *args)
    r = _run(nc, [arrays], core_ids=[0])
    return r.results[0]["out_y"]
```
